# Optimizing a Trainium2 kernel written in Bass

```python
import numpy as np
import jax
import jax.numpy as jnp

def _softmax(x, axis=-1):
    return jax.nn.softmax(x, axis=axis)

def _gelu(x):
    return jax.nn.gelu(x, approximate=True)

def _silu(x):
    return jax.nn.silu(x)

def _sigmoid(x):
    return jax.nn.sigmoid(x)

def _layernorm(x, axis=-1, eps=1e-05):
    m = jnp.mean(x, axis=axis, keepdims=True)
    v = jnp.var(x, axis=axis, keepdims=True)
    return (x - m) / jnp.sqrt(v + eps)

def _scatter_add(tgt, idx, src, axis=0):
    return tgt.at[idx].add(src)

def _segment_sum(src, seg, n):
    return jax.ops.segment_sum(src, seg, n)
kernel_name = 'mk_gnn_ffn_d1_gnn_r8_f9ee32'

def setup_inputs(seed: int=0):
    np.random.seed(seed)
    _w = jnp.asarray

    def _rec_inputs():
        import jax
        import jax.numpy as jnp
        _gk = jax.random.key(seed)
        x = -0.0003713 + 1 * jax.random.normal(jax.random.fold_in(_gk, 1), (6250, 256), jnp.float32)
        src = jax.random.randint(jax.random.fold_in(_gk, 2), (200000,), 0, 6250, jnp.int32)
        dst = jnp.minimum((6250 * jax.random.uniform(jax.random.fold_in(_gk, 3), (200000,)) ** 2.0).astype(jnp.int32), 49999)
        _o = jnp.argsort(dst, stable=True)
        src = src[_o]
        dst = dst[_o]
        edge_type_16 = jax.random.randint(jax.random.fold_in(_gk, 12), (200000,), 0, 16, jnp.int32)
        return (x, src, dst, edge_type_16)
    x, src, dst, edge_type_16 = _rec_inputs()

    def _L0_gnn_setup():
        import jax, jax.numpy as jnp
        import numpy as np
        N_NODES = 6250
        N_EDGES = 100000
        HDIM = 256
        NUMRELS = 16

        def _gru_cell(x, h, w_ih, w_hh, b_ih, b_hh):
            gi = x @ w_ih.T + b_ih
            gh = h @ w_hh.T + b_hh
            i_r, i_z, i_n = jnp.split(gi, 3, axis=-1)
            h_r, h_z, h_n = jnp.split(gh, 3, axis=-1)
            r = jax.nn.sigmoid(i_r + h_r)
            z = jax.nn.sigmoid(i_z + h_z)
            n = jnp.tanh(i_n + r * h_n)
            return (1.0 - z) * n + z * h
        key = jax.random.key(seed)
        ks = jax.random.split(key, 9)
        h = jax.random.normal(ks[0], (N_NODES, HDIM), dtype=jnp.float32)
        relvectors = jax.random.normal(ks[1], (NUMRELS, HDIM), dtype=jnp.float32)
        s = 1.0 / np.sqrt(HDIM)
        w_ih = jax.random.uniform(ks[2], (3 * HDIM, HDIM), minval=-s, maxval=s, dtype=jnp.float32)
        w_hh = jax.random.uniform(ks[3], (3 * HDIM, HDIM), minval=-s, maxval=s, dtype=jnp.float32)
        b_ih = jax.random.uniform(ks[4], (3 * HDIM,), minval=-s, maxval=s, dtype=jnp.float32)
        b_hh = jax.random.uniform(ks[5], (3 * HDIM,), minval=-s, maxval=s, dtype=jnp.float32)
        edge_src = jax.random.randint(ks[6], (N_EDGES,), 0, N_NODES, dtype=jnp.int32)
        edge_dst = jax.random.randint(ks[7], (N_EDGES,), 0, N_NODES, dtype=jnp.int32)
        edge_rel = jax.random.randint(ks[8], (N_EDGES,), 0, NUMRELS, dtype=jnp.int32)
        return {'h': h, 'relvectors': relvectors, 'w_ih': w_ih, 'w_hh': w_hh, 'b_ih': b_ih, 'b_hh': b_hh, 'edge_src': edge_src, 'edge_dst': edge_dst, 'edge_rel': edge_rel}
    _L0_gnn_all = _L0_gnn_setup()
    _L0_gnn_in = {k: v for k, v in _L0_gnn_all.items() if k in ('relvectors', 'w_ih', 'w_hh', 'b_ih', 'b_hh')}
    del _L0_gnn_all

    def _L0_ffn_setup():
        import jax, jax.numpy as jnp
        import numpy as np
        B, S, D, E, H, K = (4, 512, 256, 8, 512, 2)
        key = jax.random.key(seed)
        ks = jax.random.split(key, 6)
        x = jax.random.normal(ks[0], (B, S, D), jnp.float32)
        Wg = jax.random.normal(ks[1], (D, E), jnp.float32) * 0.02
        bg = jnp.zeros((E,), jnp.float32)
        W1 = jax.random.normal(ks[2], (E, D, H), jnp.float32) * 0.02
        b1 = jnp.zeros((E, H), jnp.float32)
        W2 = jax.random.normal(ks[3], (E, H, D), jnp.float32) * 0.02
        b2 = jnp.zeros((E, D), jnp.float32)
        return {'x': x, 'Wg': Wg, 'bg': bg, 'W1': W1, 'b1': b1, 'W2': W2, 'b2': b2}
    _L0_ffn_all = _L0_ffn_setup()
    _L0_ffn_in = {k: v for k, v in _L0_ffn_all.items() if k in ('Wg', 'bg', 'W1', 'b1', 'W2', 'b2')}
    del _L0_ffn_all
    return {'x': x, 'src': src, 'dst': dst, 'edge_type_16': edge_type_16, 'L0_gnn_relvectors': _L0_gnn_in['relvectors'], 'L0_gnn_w_ih': _L0_gnn_in['w_ih'], 'L0_gnn_w_hh': _L0_gnn_in['w_hh'], 'L0_gnn_b_ih': _L0_gnn_in['b_ih'], 'L0_gnn_b_hh': _L0_gnn_in['b_hh'], 'L0_ffn_Wg': _L0_ffn_in['Wg'], 'L0_ffn_bg': _L0_ffn_in['bg'], 'L0_ffn_W1': _L0_ffn_in['W1'], 'L0_ffn_b1': _L0_ffn_in['b1'], 'L0_ffn_W2': _L0_ffn_in['W2'], 'L0_ffn_b2': _L0_ffn_in['b2']}

def reference(x, src, dst, edge_type_16, L0_gnn_relvectors, L0_gnn_w_ih, L0_gnn_w_hh, L0_gnn_b_ih, L0_gnn_b_hh, L0_ffn_Wg, L0_ffn_bg, L0_ffn_W1, L0_ffn_b1, L0_ffn_W2, L0_ffn_b2):
    import jax
    import jax.numpy as jnp

    def _L0_gnn_ref(h, relvectors, w_ih, w_hh, b_ih, b_hh, edge_src, edge_dst, edge_rel):
        import jax, jax.numpy as jnp
        import numpy as np
        N_NODES = 6250
        N_EDGES = 100000
        HDIM = 256
        NUMRELS = 16

        def _gru_cell(x, h, w_ih, w_hh, b_ih, b_hh):
            gi = x @ w_ih.T + b_ih
            gh = h @ w_hh.T + b_hh
            i_r, i_z, i_n = jnp.split(gi, 3, axis=-1)
            h_r, h_z, h_n = jnp.split(gh, 3, axis=-1)
            r = jax.nn.sigmoid(i_r + h_r)
            z = jax.nn.sigmoid(i_z + h_z)
            n = jnp.tanh(i_n + r * h_n)
            return (1.0 - z) * n + z * h
        msg = h[edge_src] + relvectors[edge_rel]
        red = jax.ops.segment_sum(msg, edge_dst, num_segments=h.shape[0])
        return _gru_cell(red, h, w_ih, w_hh, b_ih, b_hh)

    def _L0_ffn_ref(x, Wg, bg, W1, b1, W2, b2):
        import jax, jax.numpy as jnp
        import numpy as np
        B, S, D, E, H, K = (4, 512, 256, 8, 512, 2)
        Bv, Sv, Dv = x.shape
        gate_scores = x @ Wg + bg
        _, idx = jax.lax.top_k(gate_scores, K)
        mask = jax.nn.one_hot(idx, E, dtype=x.dtype).sum(axis=-2)
        xf = x.reshape(-1, Dv)
        mf = mask.reshape(-1, E)
        h = jax.nn.gelu(jnp.einsum('td,edh->teh', xf, W1) + b1[None], approximate=False)
        y = jnp.einsum('teh,ehd->ted', h, W2) + b2[None]
        out = jnp.einsum('ted,te->td', y, mf)
        return out.reshape(Bv, Sv, Dv)
    x = x + _L0_gnn_ref(_layernorm(x, axis=-1), L0_gnn_relvectors, L0_gnn_w_ih, L0_gnn_w_hh, L0_gnn_b_ih, L0_gnn_b_hh, src, dst, edge_type_16)
    x = x + _L0_ffn_ref(_layernorm(x, axis=-1)[None], L0_ffn_Wg, L0_ffn_bg, L0_ffn_W1, L0_ffn_b1, L0_ffn_W2, L0_ffn_b2)[0]
    return x

_drawn_inputs = setup_inputs


def setup_inputs(seed=0):
    import zlib

    import numpy as np

    out = dict(_drawn_inputs(seed))
    spreads = {'L0_ffn_bg': (0.0, 0.1), 'L0_ffn_b1': (0.0, 0.374), 'L0_ffn_b2': (0.0, 0.1)}
    factors = {'L0_gnn_b_ih': 6.475, 'L0_gnn_b_hh': 7.141}
    for name, (base, spread) in spreads.items():
        noise = np.random.default_rng([zlib.crc32(name.encode()), seed]).standard_normal(out[name].shape)
        drawn = base * np.exp(spread * noise) if base else spread * noise
        out[name] = jnp.asarray(drawn.astype(out[name].dtype))
    for name, factor in factors.items():
        out[name] = (out[name] * factor).astype(out[name].dtype)
    return out
```

```python
from contextlib import ExitStack

import numpy as np
import concourse.bass as bass
from concourse import mybir

F32 = mybir.dt.float32
BF16 = mybir.dt.bfloat16
I32 = mybir.dt.int32
I16 = mybir.dt.int16
U32 = mybir.dt.uint32
ALU = mybir.AluOpType
ACT = mybir.ActivationFunctionType
AX = mybir.AxisListType.X
ds = bass.ds

N, D, E, R = 6250, 256, 200000, 16
NE, H = 8, 512
KT = D // 128
HS = H // 128
EPS = 1e-5

CH = 128
GC = 4
GE = GC * CH
WIN = 64
STEP_G = 2
SC = STEP_G * GC
STEPS = -(-E // (STEP_G * GE))
GROUPS = STEPS * STEP_G
RT = -(-GROUPS // 128)
RING = 4
IDXR = 8
LEAD = 6
PADW = -(-N // WIN)
ACOLS = PADW * WIN

SUB = 125
T = 2 * SUB
TILES = N // T
FIRST = 6
SLOTS = 8
LOOPED = (STEPS - FIRST) // SLOTS
LAST_SLOTS = (STEPS - FIRST) % SLOTS
LN_ROWS = N // 128
LN_J = 8
LN_REST = N - 128 * LN_ROWS
BIG = 1.0e6
assert N % T == 0 and LN_ROWS % LN_J == 0 and FIRST % 2 == 0 and SLOTS % IDXR == 0
assert STEPS == RING + SLOTS * ((STEPS - RING) // SLOTS) and STEPS % RING == 0
assert LOOPED == TILES - 2


def shape_constants():
    ident = np.eye(128, dtype=np.float32)
    ramp = np.tile(np.arange(WIN, dtype=np.float32), (128, 1))
    g = np.arange(RT * 128)
    a = STEPS - 1 - np.minimum(g // STEP_G, STEPS - 1)
    begun = np.where(a < FIRST, 0, (a - FIRST) // SLOTS + 1)
    limit = (N - T * np.minimum(begun, TILES - 1)).astype(np.float32).reshape(RT, 128).T
    return ident, ramp, np.ascontiguousarray(limit)


def gnn_ffn_kernel(nc, x, src, dst, etype, rel, w_ih, w_hh, b_ih, b_hh, Wg, bg, W1, b1, W2, b2,
                   c_ident, c_ramp, c_limit, out):
    h_dram = nc.dram_tensor("h_table", [N, D], F32).ap()
    x_rows = x[0:128 * LN_ROWS, :].rearrange("(p j) d -> p j d", p=128)
    h_rows = h_dram[0:128 * LN_ROWS, :].rearrange("(p j) d -> p j d", p=128)

    with ExitStack() as ctx:
        def sb(name, shape, dt=F32):
            return ctx.enter_context(nc.sbuf_tensor(name, shape, dt))

        def sem(name):
            return ctx.enter_context(nc.semaphore(name))

        ident = sb("ident", [128, 128])
        ramp = sb("ramp", [128, WIN])
        limit = sb("limit", [128, RT])
        ones = sb("ones", [128, 128])
        w1 = sb("w1", [128, NE, KT, H])
        w2 = sb("w2", [128, NE, HS, D])
        wihT = sb("wihT", [128, KT, 3 * D])
        whhT = sb("whhT", [128, KT, 3 * D])
        rels = sb("rels", [R, D])
        wg = sb("wg", [128, KT, NE])
        bgb = sb("bgb", [128, 2 * NE])
        b2s = sb("b2s", [NE, D])
        bias_rows = sb("bias_rows", [44, 128])
        bias = sb("bias", [128, 44])
        half_rz = sb("half_rz", [128, 4])
        b1c = bias[:, 0:32].rearrange("p (e s) -> p e s", e=NE)
        bihc = bias[:, 32:38]
        bhhc = bias[:, 38:44]
        src_t = sb("src_t", [128, GROUPS * GC], I16)
        dst_t = sb("dst_t", [128, GROUPS * GC], I16)
        typ_t = sb("typ_t", [128, GROUPS * GC], I16)
        base_i = sb("base_i", [1, GROUPS], I32)
        gmax = sb("gmax", [128, RT])
        gmin = sb("gmin", [128, RT])
        base = sb("base", [128, RT])
        viol = sb("viol", [128, 2, RT])
        vsum = sb("vsum", [128, 1])
        ok = sb("ok", [128, 1])
        flag = sb("flag", [1, 1], I32)
        acc = sb("acc", [128, KT, ACOLS])
        ring = sb("ring", [128, RING, SC, D])
        idx = sb("idx", [128, IDXR, SC], I32)
        onehot = sb("onehot", [128, 2, SC, WIN])
        onehot16 = sb("onehot16", [128, 2, SC, WIN], BF16)
        type16 = sb("type16", [128, 2, SC, R], BF16)
        cts = sb("cts", [R, STEP_G * WIN])
        ramp_w = sb("ramp_w", [128, WIN])
        h_in = sb("h_in", [SUB, 2, D])
        x_in = sb("x_in", [SUB, 2, D])
        hT = sb("hT", [128, KT, T])
        x1 = sb("x1", [SUB, 2, D])
        x2n = sb("x2n", [SUB, 2, D])
        x2T = sb("x2T", [128, KT, T])
        gT = sb("gT", [128, 2, HS, T])
        out_sb = sb("out_sb", [SUB, 2, D])
        scores = sb("scores", [SUB, 2, NE])
        top = sb("top", [SUB, 2, 8])
        topi = sb("topi", [SUB, 2, 8], U32)
        topf = sb("topf", [SUB, 2, 8])
        mask = sb("mask", [SUB, 2, NE])
        mask1 = sb("mask1", [SUB, 2, NE])
        maskT = sb("maskT", [NE, T])
        st = sb("st", [128, 8, 6])
        mv = sb("mv", [128, 8, 2])
        var = sb("var", [128, 8])
        std = sb("std", [128, 8])
        rstd = sb("rstd", [128, 8])
        nmr = sb("nmr", [128, 8])
        rT = gT[:, 1, 0:2, :]
        zT = gT[:, 1, 2:4, :]
        nT = gT[:, 0, 0:2, :]
        oT = gT[:, 0, 2:4, :]
        flat = acc[:, :, :].rearrange("p k n -> p (k n)")
        nat = flat[:, 0:3 * RT * GE].rearrange("p (s r e) -> p s r e", s=3, r=RT)
        nat_i = nat.bitcast(I32)
        o = 3 * RT * GE
        wnat = flat[:, o:o + 2 * 6 * D].rearrange("p (w m d) -> p w m d", w=2, m=6)
        o += 2 * 6 * D
        tmin = flat[:, o:o + RT * GE].rearrange("p (r e) -> p r e", r=RT)
        assert o + RT * GE <= KT * ACOLS
        diag = onehot[:, 0, :, :].rearrange("p a b -> p (a b)")
        base_bc = onehot[:, 1, :, :].rearrange("p a b -> p (a b)")

        P = [ctx.enter_context(nc.psum_tensor(f"P{b}", [128, 512], F32)) for b in range(8)]

        s_const = sem("s_const")
        s_ones = sem("s_ones")
        s_pads = sem("s_pads")
        s_nat = sem("s_nat")
        s_wnat = sem("s_wnat")
        s_weights = sem("s_weights")
        s_xc = [sem(f"s_xc{c}") for c in range(RING)]
        s_hst = [sem(f"s_hst{c}") for c in range(RING)]
        s_ln_var = sem("s_ln_var")
        s_ln_std = sem("s_ln_std")
        s_ln_coef = sem("s_ln_coef")
        s_ln_h = sem("s_ln_h")
        s_natf = sem("s_natf")
        s_viol = sem("s_viol")
        s_violb = sem("s_violb")
        s_diag = sem("s_diag")
        s_baseb = sem("s_baseb")
        s_based = sem("s_based")
        s_tr = sem("s_tr")
        s_trd = sem("s_trd")
        s_flag = sem("s_flag")
        s_bias = sem("s_bias")
        s_zero = sem("s_zero")
        gathered = [sem(f"gathered{r}") for r in range(RING)]
        idx_ready = sem("idx_ready")
        onehots = sem("onehots")
        s16_ready = sem("s16_ready")
        counts_done = sem("counts_done")
        cts_ready = sem("cts_ready")
        agg_done = sem("agg_done")
        acc_added = sem("acc_added")
        g_idx = sem("g_idx")
        g_type = sem("g_type")
        g_onehot = sem("g_onehot")
        g_s16 = sem("g_s16")
        g_counts = sem("g_counts")
        g_cts = sem("g_cts")
        g_agg = sem("g_agg")
        g_half = sem("g_half")
        g_added = sem("g_added")
        g_ramp = sem("g_ramp")
        h_loaded = sem("h_loaded")
        x_loaded = sem("x_loaded")
        h_trans = sem("h_trans")
        hT_ready = sem("hT_ready")
        gates_done = sem("gates_done")
        r_ready = sem("r_ready")
        pre_n = sem("pre_n")
        n_ready = sem("n_ready")
        z_ready = sem("z_ready")
        gru_ready = sem("gru_ready")
        gru_trans = sem("gru_trans")
        x1_ready = sem("x1_ready")
        var_ready = sem("var_ready")
        std_ready = sem("std_ready")
        x2n_ready = sem("x2n_ready")
        x2_trans = sem("x2_trans")
        x2T_ready = sem("x2T_ready")
        scores_done = sem("scores_done")
        mask_ready = sem("mask_ready")
        mask_trans = sem("mask_trans")
        maskT_ready = sem("maskT_ready")
        b2_done = sem("b2_done")
        b2_added = sem("b2_added")
        l1_done = sem("l1_done")
        gelu_done = sem("gelu_done")
        l2_done = sem("l2_done")
        moe_added = sem("moe_added")
        out_ready = sem("out_ready")
        stored = sem("stored")
        dve_chain = sem("dve_chain")

        def table_whole(eng):
            for r in range(RING):
                eng.wait_ge(s_hst[r], 16 * len(range(r, LN_ROWS // LN_J + 1, RING)))

        def paths(eng, fast, general):
            eng.wait_ge(s_flag, 1)
            bad = eng.value_load(flag[0:1, 0:1], min_val=0, max_val=2 * RT * 128)
            with eng.If(bad < 1):
                fast()
            with eng.Else():
                general()
            eng.end_ifs()

        def tile_loop(eng, step, tile):
            for a in range(FIRST):
                step(a, a)
            with eng.Fori(0, LOOPED) as i:
                tile(i, lambda k: step(i * SLOTS + (FIRST + k), FIRST + k))
            i = LOOPED
            tile(i, lambda k: step(i * SLOTS + FIRST + k, FIRST + k) if k < LAST_SLOTS else None)
            tile(i + 1, lambda k: None)

        def only_tiles(eng, tile):
            with eng.Fori(0, TILES) as i:
                tile(i, lambda k: None)

        block = ctx.enter_context(nc.Block())

        @block.sync
        def _(sp):
            def load_chunk(c):
                sp.dma_start(ring[:, c % RING, :, :], x_rows[:, c * LN_J:(c + 1) * LN_J, :]).then_inc(s_xc[c % RING], 16)

            load_chunk(0)
            rows = RT - 1
            whole = E // GE - rows * 128
            left = E - (rows * 128 + whole) * GE
            for n, a in enumerate((dst, src, etype)):
                sp.dma_start(nat_i[:, n, 0:rows, :],
                             a[0:rows * 128 * GE].rearrange("(r p e) -> p r e", p=128, e=GE)).then_inc(s_nat, 16)
            sp.wait_ge(s_pads, 1)
            for n, a in enumerate((dst, src, etype)):
                at = rows * 128 * GE
                sp.dma_start(nat_i[0:whole, n, rows, :],
                             a[at:at + whole * GE].rearrange("(p e) -> p e", e=GE)).then_inc(s_nat, 16)
                at += whole * GE
                sp.dma_start(nat_i[whole:whole + 1, n, rows, 0:left],
                             a[at:at + left].rearrange("(p e) -> p e", p=1)).then_inc(s_nat, 16)
            for c in range(1, RING):
                load_chunk(c)
            sp.dma_start(ident[:, :], c_ident).then_inc(s_const, 16)
            sp.dma_start(ramp[:, :], c_ramp).then_inc(s_const, 16)
            sp.dma_start(limit[:, :], c_limit).then_inc(s_const, 16)
            for c in range(LN_ROWS // LN_J):
                sp.wait_ge(s_ln_h, LN_J * (c + 1))
                sp.dma_start(h_rows[:, c * LN_J:(c + 1) * LN_J, :], ring[:, c % RING, :, :]).then_inc(s_hst[c % RING], 16)
                if c + RING < LN_ROWS // LN_J:
                    sp.wait_ge(s_hst[c % RING], 16 * (c // RING + 1))
                    load_chunk(c + RING)
            c = LN_ROWS // LN_J
            sp.wait_ge(s_hst[c % RING], 16 * (c // RING))
            sp.dma_start(ring[0:LN_REST, c % RING, 0, :], x[128 * LN_ROWS:N, :]).then_inc(s_xc[c % RING], 16)
            sp.wait_ge(s_ln_h, LN_J * c + 1)
            sp.dma_start(h_dram[128 * LN_ROWS:N, :], ring[0:LN_REST, c % RING, 0, :]).then_inc(s_hst[c % RING], 16)
            table_whole(sp)

            def node_rows(t, i):
                return t[ds(i * (-T) + (N - T), T), :].rearrange("(j p) d -> p j d", p=SUB)

            sp.dma_start(h_in[:, :, :], node_rows(h_dram, 0)).then_inc(h_loaded, 16)
            sp.dma_start(x_in[:, :, :], node_rows(x, 0)).then_inc(x_loaded, 16)
            with sp.Fori(0, TILES - 1) as i:
                sp.wait_ge(h_trans, i + 1)
                sp.dma_start(h_in[:, :, :], node_rows(h_dram, i + 1)).then_inc(h_loaded, 16)
                sp.wait_ge(x1_ready, i + 1)
                sp.dma_start(x_in[:, :, :], node_rows(x, i + 1)).then_inc(x_loaded, 16)
                sp.wait_ge(out_ready, i + 1)
                sp.dma_start(node_rows(out, i), out_sb[:, :, :]).then_inc(stored, 16)
            sp.wait_ge(out_ready, TILES)
            sp.dma_start(node_rows(out, TILES - 1), out_sb[:, :, :]).then_inc(stored, 16)
            sp.wait_ge(stored, 16 * TILES)

        @block.gpsimd
        def _(pool):
            nc.gpsimd.memset(ones[:, :], 1.0).then_inc(s_ones, 1)
            table_whole(pool)

            def gather(r, slot):
                for j in range(SC):
                    nc.gpsimd.indirect_dma_start(
                        out=ring[:, r, j, :], out_offset=None, in_=h_dram,
                        in_offset=bass.IndirectOffsetOnAxis(ap=idx[:, slot, j:j + 1], axis=0),
                    ).then_inc(gathered[r], 16)

            def fast():
                for a in range(RING):
                    pool.wait_ge(idx_ready, a + 1)
                    gather(a, a)
                with pool.Fori(0, (STEPS - RING) // SLOTS) as q:
                    for k in range(SLOTS):
                        pool.wait_ge(idx_ready, q * SLOTS + (RING + k + 1))
                        pool.wait_ge(agg_done, q * (SLOTS * STEP_G) + STEP_G * (k + 1))
                        pool.nop(nofuse=True)
                        gather(k % RING, (RING + k) % IDXR)

            def general():
                for r in range(RING):
                    pool.wait_ge(g_idx, 1)
                    gather(r, r)
                with pool.Fori(0, STEPS // RING - 1) as q:
                    pool.wait_ge(g_idx, q + 2)
                    for r in range(RING):
                        pool.wait_ge(g_agg, q * (RING * PADW) + (r + 1) * PADW)
                        pool.nop(nofuse=True)
                        gather(r, r)

            paths(pool, fast, general)

        @block.scalar
        def _(act):
            for n, w in enumerate((w_ih, w_hh)):
                act.dma_start(wnat[:, n, :, :], w.rearrange("(m p) d -> p m d", p=128)).then_inc(s_wnat, 16)
            act.dma_start(bias_rows[0:32, :], b1.rearrange("e (s p) -> (e s) p", p=128)).then_inc(s_wnat, 16)
            act.dma_start(bias_rows[32:38, :], b_ih.rearrange("(m p) -> m p", p=128)).then_inc(s_wnat, 16)
            act.dma_start(bias_rows[38:44, :], b_hh.rearrange("(m p) -> m p", p=128)).then_inc(s_wnat, 16)
            act.dma_start(rels[:, :], rel).then_inc(s_weights, 16)
            act.dma_start(wg[:, :, :], Wg.rearrange("(k p) e -> p k e", p=128)).then_inc(s_weights, 16)
            for j in range(2):
                act.dma_start(bgb[:, j * NE:(j + 1) * NE], bg.rearrange("(a e) -> a e", a=1).to_broadcast([128, NE])).then_inc(s_weights, 16)
            act.dma_start(b2s[:, :], b2).then_inc(s_weights, 16)
            act.dma_start(w1[:, :, :, :], W1.rearrange("e (k p) h -> p e k h", p=128)).then_inc(s_weights, 16)
            act.dma_start(w2[:, :, :, :], W2.rearrange("e (s p) d -> p e s d", p=128)).then_inc(s_weights, 16)

            for c in range(LN_ROWS // LN_J + 1):
                rest = c == LN_ROWS // LN_J
                nj, np_ = (1, LN_REST) if rest else (LN_J, 128)
                act.wait_ge(s_ln_var, c + 1)
                nc.scalar.activation(std[0:np_, 0:nj], var[0:np_, 0:nj], ACT.Sqrt).then_inc(s_ln_std, 1)
                act.wait_ge(s_ln_coef, c + 1)
                for j in range(nj):
                    nc.scalar.activation(ring[0:np_, c % RING, j, :], ring[0:np_, c % RING, j, :], ACT.Identity,
                                         bias=nmr[0:np_, j:j + 1], scale=rstd[0:np_, j:j + 1]).then_inc(s_ln_h, 1)

            def step(a, k):
                if not (isinstance(a, int) and a == STEPS - 1):
                    act.wait_ge(onehots, a + 2)
                    act.wait_ge(counts_done, a)
                    nc.scalar.activation(onehot16[:, (k + 1) % 2, :, :], onehot[:, (k + 1) % 2, :, :], ACT.Copy).then_inc(s16_ready, 1)
                act.wait_ge(counts_done, a + 1)
                nc.scalar.activation(cts[:, :], P[1][0:R, 256:256 + STEP_G * WIN], ACT.Copy).then_inc(cts_ready, 1)

            def tile(i, slot):
                act.wait_ge(h_trans, i + 1)
                nc.scalar.activation(hT[:, :, :].rearrange("p k t -> p (k t)"), P[6][:, 0:KT * T], ACT.Copy).then_inc(hT_ready, 1)
                slot(0)
                act.wait_ge(gates_done, i * 4 + 1)
                for m in range(2):
                    nc.scalar.activation(rT[:, m, :], P[2][:, m * T:(m + 1) * T], ACT.Tanh,
                                         bias=half_rz[:, m:m + 1], scale=0.5).then_inc(r_ready, 1)
                act.wait_ge(pre_n, i + 1)
                for m in range(2):
                    nc.scalar.activation(nT[:, m, :], oT[:, m, :], ACT.Tanh, bias=bihc[:, 4 + m:5 + m]).then_inc(n_ready, 1)
                act.wait_ge(gates_done, i * 4 + 4)
                for m in range(2):
                    nc.scalar.activation(zT[:, m, :], P[5][:, m * T:(m + 1) * T], ACT.Tanh,
                                         bias=half_rz[:, 2 + m:3 + m], scale=0.5).then_inc(z_ready, 1)
                slot(1)
                slot(2)
                act.wait_ge(var_ready, i + 1)
                nc.scalar.activation(std[0:SUB, 0:2], var[0:SUB, 0:2], ACT.Sqrt).then_inc(std_ready, 1)
                slot(3)
                act.wait_ge(x2_trans, i + 1)
                nc.scalar.activation(x2T[:, :, :].rearrange("p k t -> p (k t)"), P[6][:, 0:KT * T], ACT.Copy).then_inc(x2T_ready, 1)
                slot(4)
                for e in range(NE):
                    if e >= 2:
                        act.wait_ge(l2_done, i * NE + (e - 1))
                    for s in range(HS):
                        if s % 2 == 0:
                            act.wait_ge(l1_done, i * (2 * NE) + (2 * e + s // 2 + 1))
                        b = 2 + 2 * (e % 2) + s // 2
                        nc.scalar.activation(gT[:, e % 2, s, :], P[b][:, (s % 2) * T:(s % 2 + 1) * T], ACT.Gelu,
                                             bias=b1c[:, e, s:s + 1]).then_inc(gelu_done, 1)
                    if e == 0:
                        act.wait_ge(mask_trans, i + 1)
                        nc.scalar.activation(maskT[:, :], P[7][0:NE, 64:64 + T], ACT.Copy).then_inc(maskT_ready, 1)
                    if e in (2, 4, 6):
                        slot(4 + e // 2)

            def fast():
                act.wait_ge(onehots, 1)
                nc.scalar.activation(onehot16[:, 0, :, :], onehot[:, 0, :, :], ACT.Copy).then_inc(s16_ready, 1)
                tile_loop(act, step, tile)

            def general():
                with act.Fori(0, STEPS) as s:
                    with act.Fori(0, PADW) as w:
                        v = s * PADW + w
                        act.wait_ge(g_onehot, v + 1)
                        nc.scalar.activation(onehot16[:, 0, :, :], onehot[:, 0, :, :], ACT.Copy).then_inc(g_s16, 1)
                        act.wait_ge(g_counts, v + 1)
                        nc.scalar.activation(cts[:, :], P[1][0:R, 256:256 + STEP_G * WIN], ACT.Copy).then_inc(g_cts, 1)
                only_tiles(act, tile)

            paths(act, fast, general)

        @block.vector
        def _(dve):
            count = [0]

            def link(ins, i=0, per=0):
                count[0] += 1
                ins.then_inc(dve_chain, 1)
                dve.wait_ge(dve_chain, i * per + count[0])

            nc.vector.memset(nat[:, 1:3, RT - 1, :], 0.0)
            nc.vector.memset(nat_i[:, 0, RT - 1, :], -1).then_inc(s_pads, 1)

            def norm(c):
                rest = c == LN_ROWS // LN_J
                nj, np_ = (1, LN_REST) if rest else (LN_J, 128)
                dve.wait_ge(s_xc[c % RING], 16 * (c // RING + 1))
                for j in range(nj):
                    ins = nc.vector.bn_stats(st[0:np_, j, :], ring[0:np_, c % RING, j, :])
                link(ins)
                for j in range(nj):
                    ins = nc.vector.bn_aggr(mv[0:np_, j, :], st[0:np_, j, :])
                link(ins)
                nc.vector.tensor_scalar_add(var[0:np_, 0:nj], mv[0:np_, 0:nj, 1], EPS).then_inc(s_ln_var, 1)
                dve.wait_ge(s_ln_std, c + 1)
                if c:
                    dve.wait_ge(s_ln_h, LN_J * c)
                link(nc.vector.reciprocal(rstd[0:np_, 0:nj], std[0:np_, 0:nj]))
                nc.vector.scalar_tensor_tensor(nmr[0:np_, 0:nj], mv[0:np_, 0:nj, 0], -1.0, rstd[0:np_, 0:nj],
                                               ALU.mult, ALU.mult).then_inc(s_ln_coef, 1)

            norm(0)
            dve.wait_ge(s_nat, 16 * 9)
            link(nc.vector.tensor_copy(nat[:, 0, :, :], nat_i[:, 0, :, :]))
            nc.vector.tensor_reduce(gmax[:, :], nat[:, 0, :, :], AX, ALU.max)
            link(nc.vector.tensor_scalar(tmin[:, :, :], nat[:, 0, :, :], 0.0, BIG, ALU.is_lt, ALU.mult))
            link(nc.vector.tensor_tensor(tmin[:, :, :], tmin[:, :, :], nat[:, 0, :, :], ALU.add))
            nc.vector.tensor_reduce(gmin[:, :], tmin[:, :, :], AX, ALU.min)
            link(nc.vector.tensor_scalar(base[:, :], gmax[:, :], -float(WIN - 1), 0.0, ALU.add, ALU.max))
            dve.wait_ge(s_const, 48)
            nc.vector.tensor_tensor(viol[:, 0, :], gmin[:, :], base[:, :], ALU.is_lt)
            link(nc.vector.tensor_tensor(viol[:, 1, :], gmax[:, :], limit[:, :], ALU.is_ge))
            nc.vector.tensor_reduce(vsum[:, :], viol[:, :, :].rearrange("p a b -> p (a b)"), AX, ALU.add).then_inc(s_viol, 1)
            nc.vector.tensor_copy(nat[:, 1, :, :], nat_i[:, 1, :, :])
            nc.vector.tensor_copy(nat[:, 2, :, :], nat_i[:, 2, :, :]).then_inc(s_natf, 1)
            dve.wait_ge(s_violb, 1)
            link(nc.vector.tensor_scalar(ok[:, :], P[0][:, 0:1], 0.5, None, ALU.is_lt))
            link(nc.vector.tensor_scalar(base[:, :], base[:, :], ok[:, 0:1], None, ALU.mult))
            for r in range(RT):
                ins = nc.vector.tensor_scalar(diag[:, r * 128:(r + 1) * 128], ident[:, :], base[:, r:r + 1], None, ALU.mult)
            ins.then_inc(s_diag, 1)
            dve.wait_ge(s_baseb, 1)
            nc.vector.tensor_copy(base_i[:, :], P[1][0:1, 0:GROUPS])
            link(nc.vector.tensor_copy(base_bc[:, :], P[1][:, :]))
            norm(1)
            tables = (dst_t, src_t, typ_t)
            for n in range(3):
                for r in range(RT):
                    g = min(128, GROUPS - r * 128)
                    q = n * RT + r
                    dve.wait_ge(s_tr, q + 1)
                    o = tables[n][:, r * 128 * GC:(r * 128 + g) * GC].rearrange("p (g j) -> p g j", j=GC)
                    got = P[2 + q % 4][:, :].rearrange("p (j g) -> p g j", j=GC)[:, 0:g, :]
                    if n == 0:
                        bb = base_bc[:, r * 128:r * 128 + g].unsqueeze(2).to_broadcast([128, g, GC])
                        nc.vector.tensor_tensor(o, got, bb, ALU.subtract).then_inc(s_trd, 1)
                    else:
                        nc.vector.tensor_copy(o, got).then_inc(s_trd, 1)
                if n < 2:
                    norm(2 + n)
            link(nc.vector.tensor_copy(flag[:, :], P[0][0:1, 0:1]))
            norm(4)
            for q in range(2 * 3):
                dve.wait_ge(s_tr, 3 * RT + q + 1)
                w, m = (wihT, whhT)[q // 3], q % 3
                nc.vector.tensor_copy(w[:, :, m * 256:(m + 1) * 256],
                                      P[2 + (3 * RT + q) % 4][:, :].rearrange("p (k m) -> p k m", k=KT)).then_inc(s_trd, 1)
            dve.wait_ge(s_bias, 1)
            link(nc.vector.tensor_copy(bias[:, :], P[6][:, 0:44]))
            link(nc.vector.tensor_tensor(half_rz[:, :], bihc[:, 0:4], bhhc[:, 0:4], ALU.add))
            link(nc.vector.tensor_scalar(half_rz[:, :], half_rz[:, :], 0.5, None, ALU.mult))
            dve.wait_ge(s_tr, 3 * RT + 6)
            nc.vector.memset(acc[:, :, :], 0.0).then_inc(s_zero, 1)
            norm(5)
            norm(6)
            dve.wait_ge(s_zero, 1)
            nc.vector.memset(ok[:, :], 0.0).then_inc(s_flag, 1)
            count[0] += 0

            def lay_indices(a, slot):
                col = (a * (-SC) + (STEPS - 1) * SC) if not isinstance(a, int) else (STEPS - 1 - a) * SC
                nc.vector.tensor_copy(idx[:, slot, :], src_t[:, ds(col, SC)]).then_inc(idx_ready, 1)

            def build(a, k):
                col = (a * (-SC) + (STEPS - 1) * SC) if not isinstance(a, int) else (STEPS - 1 - a) * SC
                nc.vector.tensor_tensor(onehot[:, k % 2, :, :],
                                        dst_t[:, ds(col, SC)].unsqueeze(2).to_broadcast([128, SC, WIN]),
                                        ramp[:, :].unsqueeze(1).to_broadcast([128, SC, WIN]), ALU.is_equal)
                nc.vector.tensor_tensor(type16[:, k % 2, :, :],
                                        typ_t[:, ds(col, SC)].unsqueeze(2).to_broadcast([128, SC, R]),
                                        ramp[:, 0:R].unsqueeze(1).to_broadcast([128, SC, R]), ALU.is_equal).then_inc(onehots, 1)

            def step(a, k):
                last = isinstance(a, int) and a == STEPS - 1
                if not last:
                    dve.wait_ge(agg_done, a * STEP_G)
                    dve.wait_ge(s16_ready, a)
                    build(a + 1, k + 1)
                if not isinstance(a, int) or a + LEAD < STEPS:
                    lay_indices(a + LEAD, (k + LEAD) % IDXR)
                g0 = (a * (-STEP_G) + (STEPS - 1) * STEP_G) if not isinstance(a, int) else (STEPS - 1 - a) * STEP_G
                starts = [dve.value_load(base_i[0:1, ds(g0 + g, 1)], min_val=0, max_val=ACOLS - WIN) for g in range(STEP_G)]
                for g in range(STEP_G):
                    dve.wait_ge(agg_done, a * STEP_G + (g + 1))
                    dve.wait_ge(acc_added, a * STEP_G + g)
                    w = acc[:, :, ds(starts[g], WIN)]
                    got = P[g][:, 0:KT * WIN].rearrange("p (k n) -> p k n", k=KT)
                    nc.vector.tensor_tensor(w, got, w, ALU.add).then_inc(acc_added, 1)

            prep_links = count[0]

            def tile(i, slot):
                count[0] = prep_links

                def chain(ins, alone=False):
                    link(ins, i, LINKS)
                    if alone:
                        dve.nop(nofuse=True)

                slot(0)
                dve.wait_ge(r_ready, i * 2 + 2)
                chain(nc.vector.tensor_scalar(rT, rT, 0.5, 0.5, ALU.mult, ALU.add))
                dve.wait_ge(gates_done, i * 4 + 2)
                for m in range(2):
                    ins = nc.vector.scalar_tensor_tensor(oT[:, m, :], P[3][:, m * T:(m + 1) * T], bhhc[:, 4 + m:5 + m],
                                                         rT[:, m, :], ALU.add, ALU.mult)
                chain(ins)
                dve.wait_ge(gates_done, i * 4 + 3)
                o2 = oT.rearrange("p m t -> p (m t)")
                nc.vector.tensor_tensor(o2, P[4][:, 0:2 * T], o2, ALU.add).then_inc(pre_n, 1)
                slot(1)
                dve.wait_ge(n_ready, i * 2 + 2)
                chain(nc.vector.tensor_tensor(oT, hT[:, :, :], nT, ALU.subtract))
                dve.wait_ge(z_ready, i * 2 + 2)
                chain(nc.vector.scalar_tensor_tensor(oT, zT, 1.0, oT, ALU.add, ALU.mult))
                nc.vector.scalar_tensor_tensor(oT, oT, 0.5, nT, ALU.mult, ALU.add).then_inc(gru_ready, 1)
                slot(2)
                dve.wait_ge(gru_trans, i + 1)
                dve.wait_ge(x_loaded, i * 16 + 16)
                x1f = x1[:, :, :].rearrange("p j d -> p (j d)")
                nc.vector.tensor_tensor(x1f, P[7][0:SUB, :], x_in[:, :, :].rearrange("p j d -> p (j d)"), ALU.add).then_inc(x1_ready, 1)
                dve.wait_ge(x1_ready, i + 1)
                for j in range(2):
                    ins = nc.vector.bn_stats(st[0:SUB, j, :], x1[:, j, :])
                chain(ins, alone=True)
                for j in range(2):
                    ins = nc.vector.bn_aggr(mv[0:SUB, j, :], st[0:SUB, j, :])
                chain(ins)
                nc.vector.tensor_scalar_add(var[0:SUB, 0:2], mv[0:SUB, 0:2, 1], EPS).then_inc(var_ready, 1)
                slot(3)
                dve.wait_ge(std_ready, i + 1)
                chain(nc.vector.reciprocal(rstd[0:SUB, 0:2], std[0:SUB, 0:2]))
                for j in range(2):
                    ins = nc.vector.tensor_scalar(x2n[:, j, :], x1[:, j, :], mv[0:SUB, j, 0:1], rstd[0:SUB, j:j + 1],
                                                  ALU.subtract, ALU.mult)
                ins.then_inc(x2n_ready, 1)
                slot(4)
                dve.wait_ge(scores_done, i + 1)
                chain(nc.vector.tensor_tensor(scores[:, :, :].rearrange("p j e -> p (j e)"), P[7][0:SUB, 0:2 * NE],
                                              bgb[0:SUB, :], ALU.add), alone=True)
                for j in range(2):
                    ins = nc.vector.max(top[:, j, :], scores[:, j, :])
                chain(ins, alone=True)
                for j in range(2):
                    ins = nc.vector.max_index(topi[:, j, :], top[:, j, :], scores[:, j, :])
                chain(ins)
                chain(nc.vector.tensor_copy(topf[:, :, :], topi[:, :, :]))
                for j in range(2):
                    ins = nc.vector.tensor_scalar(mask1[:, j, :], ramp[0:SUB, 0:NE], topf[:, j, 0:1], None, ALU.is_equal)
                chain(ins)
                for j in range(2):
                    ins = nc.vector.scalar_tensor_tensor(mask[:, j, :], ramp[0:SUB, 0:NE], topf[:, j, 1:2], mask1[:, j, :],
                                                         ALU.is_equal, ALU.add)
                ins.then_inc(mask_ready, 1)
                dve.wait_ge(mask_ready, i + 1)
                dve.wait_ge(b2_done, i + 1)
                nc.vector.tensor_tensor(x1f, P[6][0:SUB, :], x1f, ALU.add).then_inc(b2_added, 1)
                dve.wait_ge(b2_added, i + 1)
                for e in range(NE):
                    dve.wait_ge(l2_done, i * NE + (e + 1))
                    if e:
                        dve.wait_ge(moe_added, i * NE + e)
                    if e == NE - 1:
                        dve.wait_ge(stored, i * 16)
                    for j in range(2):
                        to = out_sb if e == NE - 1 else x1
                        ins = nc.vector.scalar_tensor_tensor(to[:, j, :], P[7 - e % 2][0:SUB, j * D:(j + 1) * D],
                                                             mask[:, j, e:e + 1], x1[:, j, :], ALU.mult, ALU.add)
                    ins.then_inc(moe_added, 1)
                    if e == NE - 1:
                        dve.wait_ge(moe_added, i * NE + NE)
                        nc.vector.memset(ok[:, :], 0.0).then_inc(out_ready, 1)
                    if e in (1, 3, 5):
                        slot(5 + e // 2)
                assert count[0] == prep_links + LINKS, count[0] - prep_links

            LINKS = 12

            def fast():
                for a in range(LEAD):
                    lay_indices(a, a)
                build(0, 0)
                tile_loop(dve, step, tile)

            def general():
                with dve.Fori(0, STEPS // RING) as q:
                    dve.wait_ge(g_agg, q * (RING * PADW))
                    nc.vector.tensor_copy(idx[:, 0:RING, :].rearrange("p r c -> p (r c)"),
                                          src_t[:, ds(q * (RING * SC), RING * SC)]).then_inc(g_idx, 1)
                    with dve.Fori(0, RING) as r:
                        s = q * RING + r
                        nc.vector.tensor_copy(ramp_w[:, :], ramp[:, :]).then_inc(g_ramp, 1)
                        nc.vector.tensor_tensor(type16[:, 0, :, :],
                                                typ_t[:, ds(s * SC, SC)].unsqueeze(2).to_broadcast([128, SC, R]),
                                                ramp[:, 0:R].unsqueeze(1).to_broadcast([128, SC, R]), ALU.is_equal).then_inc(g_type, 1)
                        with dve.Fori(0, PADW) as w:
                            v = s * PADW + w
                            dve.wait_ge(g_ramp, s * (PADW + 1) + w + 1)
                            dve.wait_ge(g_s16, v)
                            nc.vector.tensor_tensor(onehot[:, 0, :, :],
                                                    dst_t[:, ds(s * SC, SC)].unsqueeze(2).to_broadcast([128, SC, WIN]),
                                                    ramp_w[:, :].unsqueeze(1).to_broadcast([128, SC, WIN]), ALU.is_equal).then_inc(g_onehot, 1)
                            dve.wait_ge(g_onehot, v + 1)
                            nc.vector.tensor_scalar_add(ramp_w[:, :], ramp_w[:, :], float(WIN)).then_inc(g_ramp, 1)
                            dve.wait_ge(g_agg, v + 1)
                            win = acc[:, :, ds(w * WIN, WIN)]
                            for g in range(STEP_G):
                                dve.wait_ge((g_added, g_half)[g], v + g)
                                got = P[g][:, 0:KT * WIN].rearrange("p (k n) -> p k n", k=KT)
                                nc.vector.tensor_tensor(win, got, win, ALU.add).then_inc((g_half, g_added)[g], 1)
                only_tiles(dve, tile)

            paths(dve, fast, general)

        @block.tensor
        def _(pe):
            pe.wait_ge(s_ones, 1)
            pe.wait_ge(s_viol, 1)
            nc.tensor.matmul(P[0][:, 0:1], ones[:, :], vsum[:, :], start=True, stop=True).then_inc(s_violb, 1)
            pe.wait_ge(s_diag, 1)
            nc.tensor.matmul(P[1][:, :], ones[:, :], diag, start=True, stop=True).then_inc(s_baseb, 1)
            pe.wait_ge(s_natf, 1)
            q = 0
            for n in range(3):
                for r in range(RT):
                    if q >= 4:
                        pe.wait_ge(s_trd, q - 3)
                    for j in range(GC):
                        ins = nc.tensor.transpose(P[2 + q % 4][:, j * 128:(j + 1) * 128], nat[:, n, r, j * 128:(j + 1) * 128], ident[:, :])
                    ins.then_inc(s_tr, 1)
                    q += 1
            pe.wait_ge(s_wnat, 16 * 5)
            for n in range(2):
                for m in range(3):
                    pe.wait_ge(s_trd, q - 3)
                    for k in range(KT):
                        for b in range(2):
                            at = k * 256 + b * 128
                            ins = nc.tensor.transpose(P[2 + q % 4][:, at:at + 128], wnat[:, n, 2 * m + b, k * 128:(k + 1) * 128], ident[:, :])
                    ins.then_inc(s_tr, 1)
                    q += 1
            nc.tensor.transpose(P[6][:, 0:44], bias_rows[:, :], ident[0:44, 0:44]).then_inc(s_bias, 1)
            pe.wait_ge(s_trd, q)
            pe.wait_ge(s_weights, 16 * 7)

            def products(r, k, counts_copied, group_done):
                for g in range(STEP_G):
                    for f in range(KT):
                        to = P[g][:, f * WIN:(f + 1) * WIN]
                        for j in range(GC):
                            nc.tensor.matmul(to, ring[:, r, g * GC + j, f * 128:(f + 1) * 128],
                                             onehot[:, k, g * GC + j, :], start=(j == 0), stop=False)
                        if g == 0 and f == 0:
                            counts_copied()
                        ins = nc.tensor.matmul(to, rels[:, f * 128:(f + 1) * 128], cts[:, g * WIN:(g + 1) * WIN],
                                               start=False, stop=True)
                    group_done(g, ins)

            def relation_counts(k):
                for g in range(STEP_G):
                    to = P[1][0:R, 256 + g * WIN:256 + (g + 1) * WIN]
                    for j in range(GC):
                        ins = nc.tensor.matmul(to, type16[:, k, g * GC + j, :], onehot16[:, k, g * GC + j, :],
                                               start=(j == 0), stop=(j == GC - 1))
                return ins

            def step(a, k):
                pe.wait_ge(s16_ready, a + 1)
                pe.wait_ge(acc_added, a * STEP_G)
                relation_counts(k % 2).then_inc(counts_done, 1)
                fills = a // RING + 1 if isinstance(a, int) else None
                if fills is None:
                    pe.wait_ge(gathered[k % RING], (a - k) * (16 * SC // RING) + 16 * SC * (k // RING + 1))
                else:
                    pe.wait_ge(gathered[k % RING], 16 * SC * fills)
                products(k % RING, k % 2, lambda: pe.wait_ge(cts_ready, a + 1),
                         lambda g, ins: ins.then_inc(agg_done, 1))

            def tile(i, slot):
                nb = i * (-T) + (N - T)
                pe.wait_ge(h_loaded, i * 16 + 16)
                pe.wait_ge(moe_added, i * NE)
                for k in range(KT):
                    for j in range(2):
                        at = k * T + j * SUB
                        ins = nc.tensor.transpose(P[6][:, at:at + SUB], h_in[:, j, k * 128:(k + 1) * 128], ident[0:SUB, 0:SUB])
                ins.then_inc(h_trans, 1)
                slot(0)

                def gate(bank, row, which):
                    for m in range(2):
                        to = P[bank][:, m * T:(m + 1) * T]
                        ops = [(w, k) for w in which for k in range(KT)]
                        for n, (w, k) in enumerate(ops):
                            rhs = hT[:, k, :] if w == "h" else acc[:, k, ds(nb, T)]
                            wt = whhT if w == "h" else wihT
                            ins = nc.tensor.matmul(to, wt[:, k, row + m * 128:row + (m + 1) * 128], rhs,
                                                   start=(n == 0), stop=(n == len(ops) - 1))
                    ins.then_inc(gates_done, 1)

                pe.wait_ge(hT_ready, i + 1)
                pe.wait_ge(acc_added, need_added(i))
                gate(2, 0, "hx")
                gate(3, 2 * D, "h")
                gate(4, 2 * D, "x")
                gate(5, D, "hx")
                slot(1)
                slot(2)
                pe.wait_ge(gru_ready, i + 1)
                for j in range(2):
                    for k in range(KT):
                        at = j * D + k * 128
                        ins = nc.tensor.transpose(P[7][0:SUB, at:at + 128], oT[:, k, j * SUB:(j + 1) * SUB], ident[:, :])
                ins.then_inc(gru_trans, 1)
                slot(3)
                pe.wait_ge(x2n_ready, i + 1)
                for k in range(KT):
                    for j in range(2):
                        at = k * T + j * SUB
                        ins = nc.tensor.transpose(P[6][:, at:at + SUB], x2n[:, j, k * 128:(k + 1) * 128], ident[0:SUB, 0:SUB])
                ins.then_inc(x2_trans, 1)
                slot(4)
                pe.wait_ge(x2T_ready, i + 1)
                for j in range(2):
                    for k in range(KT):
                        ins = nc.tensor.matmul(P[7][0:SUB, j * NE:(j + 1) * NE], x2T[:, k, j * SUB:(j + 1) * SUB],
                                               wg[:, k, :], start=(k == 0), stop=(k == KT - 1))
                ins.then_inc(scores_done, 1)

                def layer1(e):
                    if e >= 2:
                        pe.wait_ge(gelu_done, i * (NE * HS) + HS * (e - 1))
                    for s in range(HS):
                        to = P[2 + 2 * (e % 2) + s // 2][:, (s % 2) * T:(s % 2 + 1) * T]
                        for k in range(KT):
                            ins = nc.tensor.matmul(to, w1[:, e, k, s * 128:(s + 1) * 128], x2T[:, k, :],
                                                   start=(k == 0), stop=(k == KT - 1))
                        if s % 2:
                            ins.then_inc(l1_done, 1)

                def layer2(e):
                    pe.wait_ge(gelu_done, i * (NE * HS) + HS * (e + 1))
                    if e == 1:
                        pe.wait_ge(b2_added, i + 1)
                    if e >= 2:
                        pe.wait_ge(moe_added, i * NE + (e - 1))
                    for j in range(2):
                        to = P[7 - e % 2][0:SUB, j * D:(j + 1) * D]
                        for s in range(HS):
                            ins = nc.tensor.matmul(to, gT[:, e % 2, s, j * SUB:(j + 1) * SUB], w2[:, e, s, :],
                                                   start=(s == 0), stop=(s == HS - 1))
                    ins.then_inc(l2_done, 1)

                layer1(0)
                pe.wait_ge(mask_ready, i + 1)
                for j in range(2):
                    ins = nc.tensor.transpose(P[7][0:NE, 64 + j * SUB:64 + (j + 1) * SUB], mask[:, j, :], ident[0:SUB, 0:SUB])
                ins.then_inc(mask_trans, 1)
                layer1(1)
                pe.wait_ge(maskT_ready, i + 1)
                for j in range(2):
                    ins = nc.tensor.matmul(P[6][0:SUB, j * D:(j + 1) * D], maskT[:, j * SUB:(j + 1) * SUB], b2s[:, :],
                                           start=True, stop=True)
                ins.then_inc(b2_done, 1)
                layer2(0)
                for e in range(1, NE):
                    if e + 1 < NE:
                        layer1(e + 1)
                    layer2(e)
                    if e in (1, 3, 5):
                        slot(5 + e // 2)

            def fast():
                tile_loop(pe, step, tile)

            def general():
                with pe.Fori(0, STEPS // RING) as q:
                    for r in range(RING):
                        pe.wait_ge(gathered[r], q * (16 * SC) + 16 * SC)
                        s = q * RING + r
                        pe.wait_ge(g_type, s + 1)
                        pe.nop(nofuse=True)
                        with pe.Fori(0, PADW) as w:
                            v = s * PADW + w
                            pe.wait_ge(g_s16, v + 1)
                            pe.wait_ge(g_added, v)
                            relation_counts(0).then_inc(g_counts, 1)
                            products(r, 0, lambda: pe.wait_ge(g_cts, v + 1),
                                     lambda g, ins: ins.then_inc(g_agg, 1) if g == STEP_G - 1 else None)
                only_tiles(pe, tile)

            in_general = [False]

            def need_added(i):
                if in_general[0]:
                    return 0
                return min((FIRST + SLOTS * i), STEPS) * STEP_G if isinstance(i, int) else i * (SLOTS * STEP_G) + FIRST * STEP_G

            def general_marked():
                in_general[0] = True
                general()

            paths(pe, fast, general_marked)


_INS = ["x", "src", "dst", "edge_type_16", "L0_gnn_relvectors", "L0_gnn_w_ih", "L0_gnn_w_hh", "L0_gnn_b_ih",
        "L0_gnn_b_hh", "L0_ffn_Wg", "L0_ffn_bg", "L0_ffn_W1", "L0_ffn_b1", "L0_ffn_W2", "L0_ffn_b2"]


def kernel(**inputs):
    import numpy as _np
    import concourse.bacc as _bacc
    from concourse import mybir as _mybir
    from concourse.bass_utils import run_bass_kernel_spmd as _run

    nc = _bacc.Bacc("TRN2", target_bir_lowering=False, num_devices=1)
    arrays, args = {}, []
    named = [(n, _np.ascontiguousarray(inputs[n])) for n in _INS]
    named += list(zip(("c_ident", "c_ramp", "c_limit"), shape_constants()))
    for name, a in named:
        arrays[f"in_{name}_dram"] = a
        args.append(nc.dram_tensor(f"in_{name}_dram", a.shape, _mybir.dt.from_np(a.dtype), kind="ExternalInput").ap())
    out = nc.dram_tensor("out_0_dram", (N, D), _mybir.dt.float32, kind="ExternalOutput").ap()
    gnn_ffn_kernel(nc, *args, out)
    r = _run(nc, [arrays], core_ids=[0])
    return r.results[0]["out_0_dram"]
```

```python
from contextlib import ExitStack

import numpy as np
import concourse.bass as bass
from concourse import mybir

F32 = mybir.dt.float32
BF16 = mybir.dt.bfloat16
F16 = mybir.dt.float16
I32 = mybir.dt.int32
I16 = mybir.dt.int16
U32 = mybir.dt.uint32
ALU = mybir.AluOpType
ACT = mybir.ActivationFunctionType
AX = mybir.AxisListType.X
ds = bass.ds

N, D, E, R = 6250, 256, 200000, 16
NE, H = 8, 512
KT = D // 128
HS = H // 128
EPS = 1e-5

CH = 128
GC = 4
GE = GC * CH
WIN = 64
STEP_G = 2
SC = STEP_G * GC
STEPS = -(-E // (STEP_G * GE))
GROUPS = STEPS * STEP_G
RT = -(-GROUPS // 128)
PARTS = 3
PD = PARTS * D
RING_S = 2
RING_G = RING_S * STEP_G
IDXR = 8
LEAD = 4
PADW = -(-N // WIN)
ACOLS = PADW * WIN

SUB = 125
T = 2 * SUB
TILES = N // T
FIRST = 8
SLOTS = 8
READ_AT = 4
FIRST_READ = 6
LOOPED = (STEPS - FIRST) // SLOTS
LAST_SLOTS = (STEPS - FIRST) % SLOTS
LN_ROWS = N // 128
LN_J = 8
PAIRS = NE * H // 256
LN_CH = LN_ROWS // LN_J
LN_REST = N - 128 * LN_ROWS
XB = 4
HB = 3
BIG = 1.0e6
assert N % T == 0 and LN_ROWS % LN_J == 0 and FIRST % 2 == 0 and SLOTS % IDXR == 0
assert (STEPS - RING_S * 2) % SLOTS == 0 and STEPS % RING_S == 0 and SLOTS % (2 * RING_S) == 0
assert LOOPED == TILES - 2 and LAST_SLOTS == READ_AT


def shape_constants():
    ident = np.eye(128, dtype=np.float32)
    ramp = np.tile(np.arange(WIN, dtype=np.float32), (128, 1))
    g = np.arange(RT * 128)
    a = STEPS - 1 - np.minimum(g // STEP_G, STEPS - 1)
    reads = np.array([FIRST_READ] + [FIRST + SLOTS * i + READ_AT for i in range(TILES - 1)])
    begun = (reads[None, :] <= a[:, None]).sum(1)
    limit = (N - T * begun).astype(np.float32).reshape(RT, 128).T
    return ident, ramp, np.ascontiguousarray(limit)


def gnn_ffn_kernel(nc, x, src, dst, etype, rel, w_ih, w_hh, b_ih, b_hh, Wg, bg, W1, b1, W2, b2,
                   c_ident, c_ramp, c_limit, out):
    h_dram = nc.dram_tensor("h_table", [N, PD], BF16).ap()
    x_rows = x[0:128 * LN_ROWS, :].rearrange("(p j) d -> p j d", p=128)
    h_rows = h_dram[0:128 * LN_ROWS, :].rearrange("(p j) d -> p j d", p=128)

    with ExitStack() as ctx:
        def sb(name, shape, dt=F32):
            return ctx.enter_context(nc.sbuf_tensor(name, shape, dt))

        def sem(name):
            return ctx.enter_context(nc.semaphore(name))

        ident = sb("ident", [128, 128])
        ident16 = sb("ident16", [128, 128], BF16)
        ramp = sb("ramp", [128, WIN])
        limit = sb("limit", [128, RT])
        ones = sb("ones", [128, 128])
        w1 = sb("w1", [128, NE, KT, H])
        w2 = sb("w2", [128, NE, HS, D])
        wihT = sb("wihT", [128, KT, 3 * D])
        whhT = sb("whhT", [128, KT, 3 * D])
        rels = sb("rels", [R, PARTS, D], BF16)
        wg = sb("wg", [128, KT, NE])
        bgb = sb("bgb", [128, 2 * NE])
        b2s = sb("b2s", [NE, D])
        bias_rows = sb("bias_rows", [44, 128])
        bias = sb("bias", [128, 44])
        half_rz = sb("half_rz", [128, 4])
        b1c = bias[:, 0:32].rearrange("p (e s) -> p e s", e=NE)
        bihc = bias[:, 32:38]
        bhhc = bias[:, 38:44]
        src_t = sb("src_t", [128, GROUPS * GC], I16)
        dst_t = sb("dst_t", [128, GROUPS * GC], I16)
        typ_t = sb("typ_t", [128, GROUPS * GC], I16)
        base_i = sb("base_i", [1, GROUPS], I32)
        gmax = sb("gmax", [128, RT])
        gmin = sb("gmin", [128, RT])
        base = sb("base", [128, RT])
        viol = sb("viol", [128, 2, RT])
        vsum = sb("vsum", [128, 1])
        ok = sb("ok", [128, 1])
        flag = sb("flag", [1, 1], I32)
        acc = sb("acc", [128, KT, ACOLS])
        ring = sb("ring", [128, RING_G, GC, PD], BF16)
        idx = sb("idx", [128, IDXR, SC], I32)
        onehot = sb("onehot", [128, 2, SC, WIN], BF16)
        onetype = sb("onetype", [128, 2, SC, R], BF16)
        cts = sb("cts", [R, STEP_G * WIN], F16)
        ramp_w = sb("ramp_w", [128, WIN])
        h_in = sb("h_in", [SUB, 2, PD], BF16)
        x_in = sb("x_in", [SUB, 2, D])
        hT = sb("hT", [128, KT, T])
        x1 = sb("x1", [SUB, 2, D])
        x2n = sb("x2n", [SUB, 2, D])
        x2T = sb("x2T", [128, KT, T])
        gT = sb("gT", [128, 2, HS, T])
        rT = sb("rT", [128, KT, T])
        zT = sb("zT", [128, KT, T])
        oT = sb("oT", [128, KT, T])
        y = sb("y", [SUB, 2, D])
        out_sb = sb("out_sb", [SUB, 2, D])
        scores = sb("scores", [SUB, 2, NE])
        top = sb("top", [SUB, 2, 8])
        topi = sb("topi", [SUB, 2, 8], U32)
        topf = sb("topf", [SUB, 2, 8])
        mask = sb("mask", [SUB, 2, NE])
        mask1 = sb("mask1", [SUB, 2, NE])
        maskT = sb("maskT", [NE, T])
        st = sb("st", [128, LN_J, 6])
        mv = sb("mv", [128, 2, LN_J, 2])
        var = sb("var", [128, 2, LN_J])
        std = sb("std", [128, 2, LN_J])
        rstd = sb("rstd", [128, 2, LN_J])
        nmr = sb("nmr", [128, 2, LN_J])
        xc = w1[:, :, :, :].rearrange("p e k h -> p (e k h)").rearrange("p (c j d) -> p c j d", c=XB, j=LN_J)
        w2f = w2[:, :, :, :].rearrange("p e s d -> p (e s d)").bitcast(BF16)
        res = w2f[:, 0:2 * 2 * LN_J * D].bitcast(F32).rearrange("p (c j d) -> p c j d", c=2, j=LN_J)
        hc = [w2f[:, 4 * LN_J * D:4 * LN_J * D + LN_J * PD].rearrange("p (j q) -> p j q", j=LN_J)]
        ringf = ring[:, :, :, :].rearrange("p g c q -> p (g c q)")
        hc += [ringf[:, c * LN_J * PD:(c + 1) * LN_J * PD].rearrange("p (j q) -> p j q", j=LN_J) for c in range(2)]
        flat = acc[:, :, :].rearrange("p k n -> p (k n)")
        nat = flat[:, 0:3 * RT * GE].rearrange("p (s r e) -> p s r e", s=3, r=RT)
        nat_i = nat.bitcast(I32)
        o = 3 * RT * GE
        wnat = flat[:, o:o + 2 * 6 * D].rearrange("p (w m d) -> p w m d", w=2, m=6)
        o += 2 * 6 * D
        tmin = flat[:, o:o + GE]
        assert o + GE <= KT * ACOLS
        gflat = gT[:, :, :, :].rearrange("p b s t -> p (b s t)")
        diag = gflat[:, 0:RT * 128]
        base_bc = gflat[:, RT * 128:2 * RT * 128]

        P = [ctx.enter_context(nc.psum_tensor(f"P{b}", [128, 512], F32)) for b in range(8)]

        s_const = sem("s_const")
        s_ones = sem("s_ones")
        s_pads = sem("s_pads")
        s_nat = sem("s_nat")
        s_wnat = sem("s_wnat")
        s_weights = sem("s_weights")
        s_experts = sem("s_experts")
        s_xc = [sem(f"s_xc{c}") for c in range(XB)]
        s_hst = [sem(f"s_hst{c}") for c in range(HB)]
        s_ln_var = sem("s_ln_var")
        s_ln_std = sem("s_ln_std")
        s_ln_coef = sem("s_ln_coef")
        s_ln_h = sem("s_ln_h")
        s_part1 = sem("s_part1")
        s_rest1 = sem("s_rest1")
        s_part2 = sem("s_part2")
        s_part3 = sem("s_part3")
        s_natf = sem("s_natf")
        s_viol = sem("s_viol")
        s_violb = sem("s_violb")
        s_diag = sem("s_diag")
        s_baseb = sem("s_baseb")
        s_based = sem("s_based")
        s_tr = sem("s_tr")
        s_dst_out = sem("s_dst_out")
        s_tr_out = sem("s_tr_out")
        s_bias_out = sem("s_bias_out")
        s_flag = sem("s_flag")
        s_bias = sem("s_bias")
        s_zero = sem("s_zero")
        gathered = [sem(f"gathered{r}") for r in range(RING_G)]
        idx_ready = sem("idx_ready")
        onehots = sem("onehots")
        counts_done = sem("counts_done")
        cts_ready = sem("cts_ready")
        agg_done = sem("agg_done")
        acc_added = sem("acc_added")
        g_idx = sem("g_idx")
        g_type = sem("g_type")
        g_onehot = sem("g_onehot")
        g_counts = sem("g_counts")
        g_cts = sem("g_cts")
        g_agg = sem("g_agg")
        g_half = sem("g_half")
        g_added = sem("g_added")
        g_ramp = sem("g_ramp")
        h_loaded = sem("h_loaded")
        x_loaded = sem("x_loaded")
        h_trans = sem("h_trans")
        hT_ready = sem("hT_ready")
        hn_done = sem("hn_done")
        hn_ready = sem("hn_ready")
        r_done = sem("r_done")
        r_ready = sem("r_ready")
        rhn_ready = sem("rhn_ready")
        z_done = sem("z_done")
        z_ready = sem("z_ready")
        in_done = sem("in_done")
        pre_n = sem("pre_n")
        n_ready = sem("n_ready")
        gru_ready = sem("gru_ready")
        gru_trans = sem("gru_trans")
        x1_ready = sem("x1_ready")
        var_ready = sem("var_ready")
        std_ready = sem("std_ready")
        x2n_ready = sem("x2n_ready")
        x2_trans = sem("x2_trans")
        x2T_ready = sem("x2T_ready")
        scores_done = sem("scores_done")
        mask_ready = sem("mask_ready")
        mask_trans = sem("mask_trans")
        maskT_ready = sem("maskT_ready")
        b2_done = sem("b2_done")
        y_ready = sem("y_ready")
        l1_done = sem("l1_done")
        gelu_done = sem("gelu_done")
        l2_done = sem("l2_done")
        moe_added = sem("moe_added")
        stored = sem("stored")
        dve_chain = sem("dve_chain")

        def table_whole(eng):
            for r in range(HB):
                eng.wait_ge(s_hst[r], 16 * len(range(r, LN_CH + 1, HB)))

        def chunk_rows(c):
            return (128, LN_J) if c < LN_CH else (LN_REST, 1)

        def paths(eng, fast, general):
            eng.wait_ge(s_flag, 1)
            bad = eng.value_load(flag[0:1, 0:1], min_val=0, max_val=2 * RT * 128)
            with eng.If(bad < 1):
                fast()
            with eng.Else():
                general()
            eng.end_ifs()

        def no_steps(f, k):
            return None

        def tile_loop(eng, step, first_tile, tile):
            for a in range(FIRST_READ):
                step(a, a)
            first_tile(lambda f, k: f(FIRST_READ + k, FIRST_READ + k))
            with eng.Fori(0, LOOPED) as i:
                tile(i, lambda f, k: f(i * SLOTS + (FIRST + k), FIRST + k), True)
            i = LOOPED
            tile(i, lambda f, k: f(i * SLOTS + FIRST + k, FIRST + k) if k < LAST_SLOTS else None, True)
            tile(i + 1, no_steps, False)

        def only_tiles(eng, first_tile, tile):
            first_tile(no_steps)
            with eng.Fori(0, TILES - 1) as i:
                tile(i, no_steps, True)
            tile(TILES - 1, no_steps, False)

        block = ctx.enter_context(nc.Block())

        @block.sync
        def _(sp):
            def load_chunk(c):
                if c < LN_CH:
                    sp.dma_start(xc[:, c % XB, :, :], x_rows[:, c * LN_J:(c + 1) * LN_J, :]).then_inc(s_xc[c % XB], 16)
                else:
                    sp.dma_start(xc[0:LN_REST, c % XB, 0, :], x[128 * LN_ROWS:N, :]).then_inc(s_xc[c % XB], 16)

            load_chunk(0)
            for to, a in ((ident, c_ident), (ramp, c_ramp), (limit, c_limit)):
                sp.dma_start(to[:, :], a).then_inc(s_const, 16)
            rows = RT - 1
            whole = E // GE - rows * 128
            left = E - (rows * 128 + whole) * GE
            for n, a in enumerate((dst, src, etype)):
                sp.dma_start(nat_i[:, n, 0:rows, :],
                             a[0:rows * 128 * GE].rearrange("(r p e) -> p r e", p=128, e=GE)).then_inc(s_nat, 16)
                if n == 0:
                    sp.wait_ge(s_pads, 1)
                at = rows * 128 * GE
                sp.dma_start(nat_i[0:whole, n, rows, :],
                             a[at:at + whole * GE].rearrange("(p e) -> p e", e=GE)).then_inc(s_nat, 16)
                at += whole * GE
                sp.dma_start(nat_i[whole:whole + 1, n, rows, 0:left],
                             a[at:at + left].rearrange("(p e) -> p e", p=1)).then_inc(s_nat, 16)
                load_chunk(n + 1)
            for c in range(LN_CH + 1):
                np_, nj = chunk_rows(c)
                if c + XB <= LN_CH:
                    sp.wait_ge(s_rest1, c + 1)
                    load_chunk(c + XB)
                sp.wait_ge(s_part3, c + 1)
                if c < LN_CH:
                    sp.dma_start(h_rows[:, c * LN_J:(c + 1) * LN_J, :], hc[c % HB]).then_inc(s_hst[c % HB], 16)
                else:
                    sp.dma_start(h_dram[128 * LN_ROWS:N, :], hc[c % HB][0:LN_REST, 0, :]).then_inc(s_hst[c % HB], 16)
            table_whole(sp)

            def node_rows(t, i):
                return t[ds(i * (-T) + (N - T), T), :].rearrange("(j p) d -> p j d", p=SUB)

            sp.dma_start(h_in[:, :, :], node_rows(h_dram, 0)).then_inc(h_loaded, 16)
            sp.dma_start(x_in[:, :, :], node_rows(x, 0)).then_inc(x_loaded, 16)
            sp.dma_start(w1[:, :, :, :], W1.rearrange("e (k p) h -> p e k h", p=128)).then_inc(s_experts, 16)
            sp.dma_start(w2[:, :, :, :], W2.rearrange("e (s p) d -> p e s d", p=128)).then_inc(s_experts, 16)
            with sp.Fori(0, TILES - 1) as i:
                sp.wait_ge(h_trans, i + 1)
                sp.dma_start(h_in[:, :, :], node_rows(h_dram, i + 1)).then_inc(h_loaded, 16)
                sp.wait_ge(x1_ready, i + 1)
                sp.dma_start(x_in[:, :, :], node_rows(x, i + 1)).then_inc(x_loaded, 16)
                sp.wait_ge(moe_added, i * NE + NE)
                sp.dma_start(node_rows(out, i), out_sb[:, :, :]).then_inc(stored, 16)
            sp.wait_ge(moe_added, TILES * NE)
            sp.dma_start(node_rows(out, TILES - 1), out_sb[:, :, :]).then_inc(stored, 16)
            sp.wait_ge(stored, 16 * TILES)

        @block.gpsimd
        def _(pool):
            nc.gpsimd.memset(ones[:, :], 1.0).then_inc(s_ones, 1)
            for c in range(LN_CH + 1):
                np_, nj = chunk_rows(c)
                pool.wait_ge(s_part1, c + 1)
                if c >= 2:
                    pool.wait_ge(s_part3, c - 1)
                nc.gpsimd.tensor_tensor(res[0:np_, c % 2, 0:nj, :], xc[0:np_, c % XB, 0:nj, :],
                                        hc[c % HB][0:np_, 0:nj, 0:D], ALU.subtract).then_inc(s_rest1, 1)
            pool.wait_ge(s_tr, 3 * RT + 6)
            nc.gpsimd.memset(acc[:, 0, :], 0.0).then_inc(s_zero, 1)
            table_whole(pool)

            def gather(r, slot, g):
                for j in range(GC):
                    nc.gpsimd.indirect_dma_start(
                        out=ring[:, r, j, :], out_offset=None, in_=h_dram,
                        in_offset=bass.IndirectOffsetOnAxis(ap=idx[:, slot, g * GC + j:g * GC + j + 1], axis=0),
                    ).then_inc(gathered[r], 16)

            def fast():
                for a in range(2 * RING_S):
                    pool.wait_ge(idx_ready, a + 1)
                    for g in range(STEP_G):
                        n = a * STEP_G + g
                        if n >= RING_G:
                            pool.wait_ge(agg_done, n - RING_G + 1)
                        gather(n % RING_G, a, g)
                with pool.Fori(0, (STEPS - 2 * RING_S) // SLOTS) as q:
                    for k in range(SLOTS):
                        pool.wait_ge(idx_ready, q * SLOTS + (2 * RING_S + k + 1))
                        for g in range(STEP_G):
                            n = (2 * RING_S + k) * STEP_G + g
                            pool.wait_ge(agg_done, q * (SLOTS * STEP_G) + (n - RING_G + 1))
                            pool.nop(nofuse=True)
                            gather(n % RING_G, (2 * RING_S + k) % IDXR, g)

            def general():
                pool.wait_ge(g_idx, 1)
                for r in range(RING_S):
                    for g in range(STEP_G):
                        gather(r * STEP_G + g, r, g)
                with pool.Fori(0, STEPS // RING_S - 1) as q:
                    pool.wait_ge(g_idx, q + 2)
                    for r in range(RING_S):
                        pool.wait_ge(g_agg, q * (RING_S * PADW) + (r + 1) * PADW)
                        pool.nop(nofuse=True)
                        for g in range(STEP_G):
                            gather(r * STEP_G + g, r, g)

            paths(pool, fast, general)

        @block.scalar
        def _(act):
            for n, w in enumerate((w_ih, w_hh)):
                act.dma_start(wnat[:, n, :, :], w.rearrange("(m p) d -> p m d", p=128)).then_inc(s_wnat, 16)
            act.dma_start(bias_rows[0:32, :], b1.rearrange("e (s p) -> (e s) p", p=128)).then_inc(s_wnat, 16)
            act.dma_start(bias_rows[32:38, :], b_ih.rearrange("(m p) -> m p", p=128)).then_inc(s_wnat, 16)
            act.dma_start(bias_rows[38:44, :], b_hh.rearrange("(m p) -> m p", p=128)).then_inc(s_wnat, 16)
            act.dma_start(y[0:R, 0, :], rel).then_inc(s_weights, 16)
            act.dma_start(wg[:, :, :], Wg.rearrange("(k p) e -> p k e", p=128)).then_inc(s_weights, 16)
            for j in range(2):
                act.dma_start(bgb[:, j * NE:(j + 1) * NE], bg.rearrange("(a e) -> a e", a=1).to_broadcast([128, NE])).then_inc(s_weights, 16)
            act.dma_start(b2s[:, :], b2).then_inc(s_weights, 16)

            act.wait_ge(s_nat, 16 * 9)
            for n in (1, 2):
                nc.scalar.activation(nat[:, n, :, :], nat_i[:, n, :, :], ACT.Copy).then_inc(s_natf, 1)
            outs = []

            def part2(c):
                np_, nj = chunk_rows(c)
                act.wait_ge(s_rest1, c + 1)
                nc.scalar.activation(hc[c % HB][0:np_, 0:nj, D:2 * D], res[0:np_, c % 2, 0:nj, :], ACT.Copy).then_inc(s_part2, 1)

            def out_table(q):
                n, r = divmod(q, RT)
                g = min(128, GROUPS - r * 128)
                act.wait_ge(s_tr, q + 1)
                o = (dst_t, src_t, typ_t)[n][:, r * 128 * GC:(r * 128 + g) * GC].rearrange("p (g j) -> p g j", j=GC)
                nc.scalar.activation(o, P[2 + q % 4][:, :].rearrange("p (j g) -> p g j", j=GC)[:, 0:g, :], ACT.Copy).then_inc(s_tr_out, 1)

            def out_weights(q):
                act.wait_ge(s_tr, 3 * RT + q + 1)
                w, m = (wihT, whhT)[q // 3], q % 3
                nc.scalar.activation(w[:, :, m * 256:(m + 1) * 256],
                                     P[2 + (3 * RT + q) % 4][:, :].rearrange("p (k m) -> p k m", k=KT), ACT.Copy).then_inc(s_tr_out, 1)

            for c in range(LN_CH + 1):
                np_, nj = chunk_rows(c)
                act.wait_ge(s_ln_var, c + 1)
                nc.scalar.activation(std[0:np_, c % 2, 0:nj], var[0:np_, c % 2, 0:nj], ACT.Sqrt).then_inc(s_ln_std, 1)
                if c:
                    part2(c - 1)
                act.wait_ge(s_ln_coef, c + 1)
                for j in range(nj):
                    ins = nc.scalar.activation(xc[0:np_, c % XB, j, :], xc[0:np_, c % XB, j, :], ACT.Identity,
                                               bias=nmr[0:np_, c % 2, j:j + 1], scale=rstd[0:np_, c % 2, j:j + 1])
                ins.then_inc(s_ln_h, 1)
                act.wait_ge(s_ln_h, c + 1)
                if c >= HB:
                    act.wait_ge(s_hst[c % HB], 16 * (c // HB))
                nc.scalar.activation(hc[c % HB][0:np_, 0:nj, 0:D], xc[0:np_, c % XB, 0:nj, :], ACT.Copy).then_inc(s_part1, 1)
                if c in (2, 3):
                    for r in range(RT):
                        out_table((c - 1) * RT + r)
                if c in (4, 5):
                    for q in range(3):
                        out_weights((c - 4) * 3 + q)
            part2(LN_CH)

            def step(a, k):
                if not (isinstance(a, int) and a == STEPS - 1):
                    act.wait_ge(counts_done, a + 2)
                    nc.scalar.activation(cts[:, :], P[0][0:R, 256:256 + STEP_G * WIN], ACT.Copy).then_inc(cts_ready, 1)

            b5 = P[5][:, 0:KT * T]

            def copy_hT(t):
                act.wait_ge(h_trans, t + 1)
                act.wait_ge(gru_ready, t)
                nc.scalar.activation(hT[:, :, :].rearrange("p k t -> p (k t)"), b5, ACT.Copy).then_inc(hT_ready, 1)

            def bias_hn(t):
                act.wait_ge(hn_done, t + 1)
                act.wait_ge(gru_trans, t)
                for m in range(KT):
                    ins = nc.scalar.activation(oT[:, m, :], b5[:, m * T:(m + 1) * T], ACT.Identity, bias=bhhc[:, 4 + m:5 + m])
                ins.then_inc(hn_ready, 1)

            def gate_r(t):
                act.wait_ge(r_done, t + 1)
                for m in range(KT):
                    ins = nc.scalar.activation(rT[:, m, :], b5[:, m * T:(m + 1) * T], ACT.Tanh,
                                               bias=half_rz[:, m:m + 1], scale=0.5)
                ins.then_inc(r_ready, 1)

            def gate_z(t):
                act.wait_ge(z_done, t + 1)
                for m in range(KT):
                    ins = nc.scalar.activation(zT[:, m, :], b5[:, m * T:(m + 1) * T], ACT.Tanh,
                                               bias=half_rz[:, 2 + m:3 + m], scale=0.5)
                ins.then_inc(z_ready, 1)

            def gate_n(t):
                act.wait_ge(pre_n, t + 1)
                for m in range(KT):
                    ins = nc.scalar.activation(rT[:, m, :], oT[:, m, :], ACT.Tanh, bias=bihc[:, 4 + m:5 + m])
                ins.then_inc(n_ready, 1)

            def root(t):
                act.wait_ge(var_ready, t + 1)
                nc.scalar.activation(std[0:SUB, 0, 0:2], var[0:SUB, 0, 0:2], ACT.Sqrt).then_inc(std_ready, 1)

            def copy_x2T(t):
                act.wait_ge(x2_trans, t + 1)
                nc.scalar.activation(x2T[:, :, :].rearrange("p k t -> p (k t)"), b5, ACT.Copy).then_inc(x2T_ready, 1)

            def first_tile(run):
                copy_hT(0)
                bias_hn(0)
                gate_r(0)
                gate_z(0)
                run(step, 0)
                gate_n(0)
                run(step, 1)
                root(0)
                copy_x2T(0)

            def tile(i, run, more):
                def gelu(e):
                    act.wait_ge(l2_done, i * NE + (e - 1) if e >= 2 else i * NE)
                    for s in range(HS):
                        p = e * (HS // 2) + s // 2
                        if s % 2 == 0:
                            act.wait_ge(l1_done, i * PAIRS + (p + 1))
                        ins = nc.scalar.activation(gT[:, e % 2, s, :], P[2 + p % 3][:, (s % 2) * T:(s % 2 + 1) * T], ACT.Gelu,
                                                   bias=b1c[:, e, s:s + 1])
                        if s % 2:
                            ins.then_inc(gelu_done, 1)

                gelu(0)
                act.wait_ge(mask_trans, i + 1)
                nc.scalar.activation(maskT[:, :], P[5][0:NE, 64:64 + T], ACT.Copy).then_inc(maskT_ready, 1)
                gelu(1)
                run(step, 0)
                for e in range(1, NE):
                    if e + 1 < NE:
                        gelu(e + 1)
                    if more and e == 1:
                        copy_hT(i + 1)
                    if more and e == 2:
                        bias_hn(i + 1)
                    if more and e == 4:
                        gate_r(i + 1)
                    if more and e == 5:
                        gate_n(i + 1)
                    if more and e == 6:
                        root(i + 1)
                    if more and e == 7:
                        copy_x2T(i + 1)
                    run(step, e)
                    if more and e == 4:
                        gate_z(i + 1)

            def fast():
                act.wait_ge(counts_done, 1)
                nc.scalar.activation(cts[:, :], P[0][0:R, 256:256 + STEP_G * WIN], ACT.Copy).then_inc(cts_ready, 1)
                tile_loop(act, step, first_tile, tile)

            def general():
                with act.Fori(0, STEPS) as s:
                    with act.Fori(0, PADW) as w:
                        act.wait_ge(g_counts, s * PADW + w + 1)
                        nc.scalar.activation(cts[:, :], P[0][0:R, 256:256 + STEP_G * WIN], ACT.Copy).then_inc(g_cts, 1)
                only_tiles(act, first_tile, tile)

            paths(act, fast, general)

        @block.vector
        def _(dve):
            count = [0]

            at = [0]
            LINKS = 10

            def link(ins, alone=False):
                count[0] += 1
                ins.then_inc(dve_chain, 1)
                dve.wait_ge(dve_chain, at[0] * LINKS + count[0])
                if alone:
                    dve.nop(nofuse=True)

            nc.vector.memset(nat[:, 1:3, RT - 1, :], 0.0)
            nc.vector.memset(nat_i[:, 0, RT - 1, :], -1).then_inc(s_pads, 1)

            def statistics(c):
                np_, nj = chunk_rows(c)
                b = c % 2
                dve.wait_ge(s_xc[c % XB], 16 * (c // XB + 1))
                for j in range(nj):
                    ins = nc.vector.bn_stats(st[0:np_, j, :], xc[0:np_, c % XB, j, :])
                link(ins)
                for j in range(nj):
                    ins = nc.vector.bn_aggr(mv[0:np_, b, j, :], st[0:np_, j, :])
                link(ins)
                nc.vector.tensor_scalar_add(var[0:np_, b, 0:nj], mv[0:np_, b, 0:nj, 1], EPS).then_inc(s_ln_var, 1)

            def coefficients(c):
                np_, nj = chunk_rows(c)
                b = c % 2
                dve.wait_ge(s_ln_std, c + 1)
                if c >= 2:
                    dve.wait_ge(s_ln_h, c - 1)
                link(nc.vector.reciprocal(rstd[0:np_, b, 0:nj], std[0:np_, b, 0:nj]))
                nc.vector.scalar_tensor_tensor(nmr[0:np_, b, 0:nj], mv[0:np_, b, 0:nj, 0], -1.0, rstd[0:np_, b, 0:nj],
                                               ALU.mult, ALU.mult).then_inc(s_ln_coef, 1)
                dve.wait_ge(s_ln_coef, c + 1)

            def part3(c):
                np_, nj = chunk_rows(c)
                dve.wait_ge(s_part2, c + 1)
                nc.vector.tensor_tensor(hc[c % HB][0:np_, 0:nj, 2 * D:PD], res[0:np_, c % 2, 0:nj, :],
                                        hc[c % HB][0:np_, 0:nj, D:2 * D], ALU.subtract).then_inc(s_part3, 1)

            statistics(0)
            statistics(1)
            coefficients(0)
            dve.wait_ge(s_nat, 16 * 9)
            link(nc.vector.tensor_copy(nat[:, 0, :, :], nat_i[:, 0, :, :]))
            nc.vector.tensor_reduce(gmax[:, :], nat[:, 0, :, :], AX, ALU.max)
            link(nc.vector.tensor_scalar(tmin[:, :], nat[:, 0, RT - 1, :], 0.0, BIG, ALU.is_lt, ALU.mult))
            link(nc.vector.tensor_tensor(tmin[:, :], tmin[:, :], nat[:, 0, RT - 1, :], ALU.add))
            nc.vector.tensor_reduce(gmin[:, RT - 1:RT], tmin[:, :], AX, ALU.min)
            nc.vector.tensor_reduce(gmin[:, 0:RT - 1], nat[:, 0, 0:RT - 1, :], AX, ALU.min)
            link(nc.vector.tensor_scalar(base[:, :], gmax[:, :], -float(WIN - 1), 0.0, ALU.add, ALU.max))
            dve.wait_ge(s_const, 48)
            nc.vector.tensor_tensor(viol[:, 0, :], gmin[:, :], base[:, :], ALU.is_lt)
            link(nc.vector.tensor_tensor(viol[:, 1, :], gmax[:, :], limit[:, :], ALU.is_ge))
            nc.vector.tensor_reduce(vsum[:, :], viol[:, :, :].rearrange("p a b -> p (a b)"), AX, ALU.add).then_inc(s_viol, 1)
            coefficients(1)
            statistics(2)
            dve.wait_ge(s_violb, 1)
            link(nc.vector.tensor_scalar(ok[:, :], P[0][:, 0:1], 0.5, None, ALU.is_lt))
            link(nc.vector.tensor_scalar(base[:, :], base[:, :], ok[:, 0:1], None, ALU.mult))
            for r in range(RT):
                ins = nc.vector.tensor_scalar(diag[:, r * 128:(r + 1) * 128], ident[:, :], base[:, r:r + 1], None, ALU.mult)
            ins.then_inc(s_diag, 1)
            part3(0)
            coefficients(2)
            statistics(3)
            dve.wait_ge(s_baseb, 1)
            nc.vector.tensor_copy(base_i[:, :], P[1][0:1, 0:GROUPS])
            link(nc.vector.tensor_copy(base_bc[:, :], P[1][:, :]))
            for r in range(RT):
                g = min(128, GROUPS - r * 128)
                dve.wait_ge(s_tr, r + 1)
                nc.vector.tensor_tensor(dst_t[:, r * 128 * GC:(r * 128 + g) * GC].rearrange("p (g j) -> p g j", j=GC),
                                        P[2 + r % 4][:, :].rearrange("p (j g) -> p g j", j=GC)[:, 0:g, :],
                                        base_bc[:, r * 128:r * 128 + g].unsqueeze(2).to_broadcast([128, g, GC]),
                                        ALU.subtract).then_inc(s_dst_out, 1)
            part3(1)
            coefficients(3)
            link(nc.vector.tensor_copy(flag[:, :], P[0][0:1, 0:1]))
            for c in range(4, LN_CH + 1):
                statistics(c)
                part3(c - 2)
                coefficients(c)
            dve.wait_ge(s_weights, 16 * 5)
            raw, rest = y[0:R, 0, :], y[0:R, 1, :]
            link(nc.vector.tensor_copy(rels[:, 0, :], raw))
            link(nc.vector.tensor_tensor(rest, raw, rels[:, 0, :], ALU.subtract))
            link(nc.vector.tensor_copy(rels[:, 1, :], rest))
            link(nc.vector.tensor_tensor(rels[:, 2, :], rest, rels[:, 1, :], ALU.subtract))
            link(nc.vector.tensor_copy(ident16[:, :], ident[:, :]))
            part3(LN_CH - 1)
            dve.wait_ge(s_bias, 1)
            link(nc.vector.tensor_copy(bias[:, :], P[6][:, 0:44]))
            link(nc.vector.tensor_tensor(half_rz[:, :], bihc[:, 0:4], bhhc[:, 0:4], ALU.add))
            link(nc.vector.tensor_scalar(half_rz[:, :], half_rz[:, :], 0.5, None, ALU.mult))
            part3(LN_CH)
            dve.wait_ge(s_tr, 3 * RT + 6)
            nc.vector.memset(acc[:, 1, :], 0.0).then_inc(s_zero, 1)
            dve.wait_ge(s_zero, 2)
            dve.wait_ge(s_tr_out, 2 * RT)
            link(nc.vector.memset(ok[:, :], 0.0))
            nc.vector.memset(ok[:, :], 0.0).then_inc(s_flag, 1)

            def lay_indices(a, slot):
                col = (a * (-SC) + (STEPS - 1) * SC) if not isinstance(a, int) else (STEPS - 1 - a) * SC
                nc.vector.tensor_copy(idx[:, slot, :], src_t[:, ds(col, SC)]).then_inc(idx_ready, 1)

            def build(a, k):
                col = (a * (-SC) + (STEPS - 1) * SC) if not isinstance(a, int) else (STEPS - 1 - a) * SC
                nc.vector.tensor_tensor(onehot[:, k % 2, :, :],
                                        dst_t[:, ds(col, SC)].unsqueeze(2).to_broadcast([128, SC, WIN]),
                                        ramp[:, :].unsqueeze(1).to_broadcast([128, SC, WIN]), ALU.is_equal)
                nc.vector.tensor_tensor(onetype[:, k % 2, :, :],
                                        typ_t[:, ds(col, SC)].unsqueeze(2).to_broadcast([128, SC, R]),
                                        ramp[:, 0:R].unsqueeze(1).to_broadcast([128, SC, R]), ALU.is_equal).then_inc(onehots, 1)

            def step(a, k):
                last = isinstance(a, int) and a == STEPS - 1
                if not last:
                    dve.wait_ge(agg_done, a * STEP_G)
                    build(a + 1, k + 1)
                if not isinstance(a, int) or a + LEAD < STEPS:
                    lay_indices(a + LEAD, (k + LEAD) % IDXR)
                g0 = (a * (-STEP_G) + (STEPS - 1) * STEP_G) if not isinstance(a, int) else (STEPS - 1 - a) * STEP_G
                starts = [dve.value_load(base_i[0:1, ds(g0 + g, 1)], min_val=0, max_val=ACOLS - WIN) for g in range(STEP_G)]
                for g in range(STEP_G):
                    dve.wait_ge(agg_done, a * STEP_G + (g + 1))
                    dve.wait_ge(acc_added, a * STEP_G + g)
                    w = acc[:, :, ds(starts[g], WIN)]
                    got = P[g][:, 0:KT * WIN].rearrange("p (k n) -> p k n", k=KT)
                    nc.vector.tensor_tensor(w, got, w, ALU.add).then_inc(acc_added, 1)

            def add_rhn(t):
                dve.wait_ge(r_ready, t + 1)
                dve.wait_ge(hn_ready, t + 1)
                nc.vector.scalar_tensor_tensor(oT[:, :, :], rT[:, :, :], 1.0, oT[:, :, :], ALU.add, ALU.mult).then_inc(rhn_ready, 1)

            def add_in(t):
                dve.wait_ge(rhn_ready, t + 1)
                dve.wait_ge(in_done, t + 1)
                flat_o = oT[:, :, :].rearrange("p m t -> p (m t)")
                nc.vector.scalar_tensor_tensor(flat_o, flat_o, 0.5, P[5][:, 0:KT * T], ALU.mult, ALU.add).then_inc(pre_n, 1)

            def blend(t):
                dve.wait_ge(n_ready, t + 1)
                dve.wait_ge(z_ready, t + 1)
                link(nc.vector.tensor_tensor(oT[:, :, :], hT[:, :, :], rT[:, :, :], ALU.subtract))
                link(nc.vector.scalar_tensor_tensor(oT[:, :, :], zT[:, :, :], 1.0, oT[:, :, :], ALU.add, ALU.mult))
                nc.vector.scalar_tensor_tensor(oT[:, :, :], oT[:, :, :], 0.5, rT[:, :, :], ALU.mult, ALU.add).then_inc(gru_ready, 1)

            def residual(t):
                dve.wait_ge(gru_trans, t + 1)
                dve.wait_ge(x_loaded, t * 16 + 16)
                nc.vector.tensor_tensor(x1[:, :, :].rearrange("p j d -> p (j d)"), P[5][0:SUB, :],
                                        x_in[:, :, :].rearrange("p j d -> p (j d)"), ALU.add).then_inc(x1_ready, 1)
                dve.wait_ge(x1_ready, t + 1)
                for j in range(2):
                    ins = nc.vector.bn_stats(st[0:SUB, j, :], x1[:, j, :])
                link(ins, alone=True)
                for j in range(2):
                    ins = nc.vector.bn_aggr(mv[0:SUB, 0, j, :], st[0:SUB, j, :])
                link(ins)
                nc.vector.tensor_scalar_add(var[0:SUB, 0, 0:2], mv[0:SUB, 0, 0:2, 1], EPS).then_inc(var_ready, 1)

            def second_norm(t):
                dve.wait_ge(std_ready, t + 1)
                dve.wait_ge(x2_trans, t)
                link(nc.vector.reciprocal(rstd[0:SUB, 0, 0:2], std[0:SUB, 0, 0:2]))
                for j in range(2):
                    ins = nc.vector.tensor_scalar(x2n[:, j, :], x1[:, j, :], mv[0:SUB, 0, j, 0:1], rstd[0:SUB, 0, j:j + 1],
                                                  ALU.subtract, ALU.mult)
                ins.then_inc(x2n_ready, 1)

            def first_tile(run):
                add_rhn(0)
                run(step, 0)
                add_in(0)
                blend(0)
                run(step, 1)
                residual(0)
                second_norm(0)
                links_before[0] = count[0]

            def tile(i, run, more):
                count[0] = links_before[0]
                at[0] = i
                dve.wait_ge(moe_added, i * NE)
                dve.wait_ge(scores_done, i + 1)
                link(nc.vector.tensor_tensor(scores[:, :, :].rearrange("p j e -> p (j e)"), P[5][0:SUB, 0:2 * NE],
                                             bgb[0:SUB, :], ALU.add), alone=True)
                for j in range(2):
                    ins = nc.vector.max(top[:, j, :], scores[:, j, :])
                link(ins, alone=True)
                for j in range(2):
                    ins = nc.vector.max_index(topi[:, j, :], top[:, j, :], scores[:, j, :])
                link(ins)
                link(nc.vector.tensor_copy(topf[:, :, :], topi[:, :, :]))
                for j in range(2):
                    ins = nc.vector.tensor_scalar(mask1[:, j, :], ramp[0:SUB, 0:NE], topf[:, j, 0:1], None, ALU.is_equal)
                link(ins)
                for j in range(2):
                    ins = nc.vector.scalar_tensor_tensor(mask[:, j, :], ramp[0:SUB, 0:NE], topf[:, j, 1:2], mask1[:, j, :],
                                                         ALU.is_equal, ALU.add)
                ins.then_inc(mask_ready, 1)
                dve.wait_ge(mask_ready, i + 1)

                def add_expert(e):
                    dve.wait_ge(l2_done, i * NE + (e + 1))
                    if e:
                        dve.wait_ge(moe_added, i * NE + e)
                    if e == NE - 1:
                        dve.wait_ge(stored, i * 16)
                    for j in range(2):
                        to = out_sb if e == NE - 1 else y
                        ins = nc.vector.scalar_tensor_tensor(to[:, j, :], P[7 - e % 2][0:SUB, j * D:(j + 1) * D],
                                                             mask[:, j, e:e + 1], y[:, j, :], ALU.mult, ALU.add)
                    ins.then_inc(moe_added, 1)

                run(step, 0)
                dve.wait_ge(b2_done, i + 1)
                nc.vector.tensor_tensor(y[:, :, :].rearrange("p j d -> p (j d)"), P[5][0:SUB, :],
                                        x1[:, :, :].rearrange("p j d -> p (j d)"), ALU.add).then_inc(y_ready, 1)
                dve.wait_ge(y_ready, i + 1)
                add_expert(0)
                for e in range(1, NE):
                    if more and e == 5:
                        add_in(i + 1)
                    if more and e == 6:
                        residual(i + 1)
                    run(step, e)
                    if more and e == 4:
                        add_rhn(i + 1)
                    if more and e == 5:
                        blend(i + 1)
                    if more and e == 6:
                        second_norm(i + 1)
                    add_expert(e)
                assert not more or count[0] == links_before[0] + LINKS, count[0] - links_before[0]

            links_before = [0]

            def fast():
                for a in range(LEAD):
                    lay_indices(a, a)
                build(0, 0)
                tile_loop(dve, step, first_tile, tile)

            def general():
                with dve.Fori(0, STEPS // RING_S) as q:
                    dve.wait_ge(g_agg, q * (RING_S * PADW))
                    nc.vector.tensor_copy(idx[:, 0:RING_S, :].rearrange("p r c -> p (r c)"),
                                          src_t[:, ds(q * (RING_S * SC), RING_S * SC)]).then_inc(g_idx, 1)
                    with dve.Fori(0, RING_S) as r:
                        s = q * RING_S + r
                        nc.vector.tensor_copy(ramp_w[:, :], ramp[:, :]).then_inc(g_ramp, 1)
                        nc.vector.tensor_tensor(onetype[:, 0, :, :],
                                                typ_t[:, ds(s * SC, SC)].unsqueeze(2).to_broadcast([128, SC, R]),
                                                ramp[:, 0:R].unsqueeze(1).to_broadcast([128, SC, R]), ALU.is_equal).then_inc(g_type, 1)
                        with dve.Fori(0, PADW) as w:
                            v = s * PADW + w
                            dve.wait_ge(g_ramp, s * (PADW + 1) + w + 1)
                            nc.vector.tensor_tensor(onehot[:, 0, :, :],
                                                    dst_t[:, ds(s * SC, SC)].unsqueeze(2).to_broadcast([128, SC, WIN]),
                                                    ramp_w[:, :].unsqueeze(1).to_broadcast([128, SC, WIN]), ALU.is_equal).then_inc(g_onehot, 1)
                            dve.wait_ge(g_onehot, v + 1)
                            nc.vector.tensor_scalar_add(ramp_w[:, :], ramp_w[:, :], float(WIN)).then_inc(g_ramp, 1)
                            dve.wait_ge(g_agg, v + 1)
                            win = acc[:, :, ds(w * WIN, WIN)]
                            for g in range(STEP_G):
                                dve.wait_ge((g_added, g_half)[g], v + g)
                                got = P[g][:, 0:KT * WIN].rearrange("p (k n) -> p k n", k=KT)
                                nc.vector.tensor_tensor(win, got, win, ALU.add).then_inc((g_half, g_added)[g], 1)
                count[0] = links_prep
                at[0] = 0
                only_tiles(dve, first_tile, tile)

            links_prep = count[0]
            paths(dve, fast, general)

        @block.tensor
        def _(pe):
            pe.wait_ge(s_ones, 1)
            pe.wait_ge(s_viol, 1)
            nc.tensor.matmul(P[0][:, 0:1], ones[:, :], vsum[:, :], start=True, stop=True).then_inc(s_violb, 1)
            pe.wait_ge(s_diag, 1)
            nc.tensor.matmul(P[1][:, :], ones[:, :], diag, start=True, stop=True).then_inc(s_baseb, 1)
            q = 0

            def bank_free(q):
                if q >= 4:
                    pe.wait_ge(s_dst_out if q < 4 + RT else s_tr_out, q - 3 if q < 4 + RT else q - 3 - RT)

            for n in range(3):
                if n:
                    pe.wait_ge(s_natf, n)
                for r in range(RT):
                    bank_free(q)
                    for j in range(GC):
                        ins = nc.tensor.transpose(P[2 + q % 4][:, j * 128:(j + 1) * 128], nat[:, n, r, j * 128:(j + 1) * 128], ident[:, :])
                    ins.then_inc(s_tr, 1)
                    q += 1
            pe.wait_ge(s_wnat, 16 * 5)
            for n in range(2):
                for m in range(3):
                    bank_free(q)
                    for k in range(KT):
                        for b in range(2):
                            at = k * 256 + b * 128
                            ins = nc.tensor.transpose(P[2 + q % 4][:, at:at + 128], wnat[:, n, 2 * m + b, k * 128:(k + 1) * 128], ident[:, :])
                    ins.then_inc(s_tr, 1)
                    q += 1
            nc.tensor.transpose(P[6][:, 0:44], bias_rows[:, :], ident[0:44, 0:44]).then_inc(s_bias, 1)
            pe.wait_ge(s_tr_out, q - RT)
            pe.wait_ge(s_weights, 16 * 5)

            def products(r, k, g):
                for f in range(KT):
                    to = P[g][:, f * WIN:(f + 1) * WIN]
                    for part in range(PARTS):
                        at = part * D + f * 128
                        for j in range(GC):
                            nc.tensor.matmul(to, ring[:, r * STEP_G + g, j, at:at + 128], onehot[:, k, g * GC + j, :],
                                             start=(part == 0 and j == 0), stop=False)
                    for part in range(PARTS):
                        ins = nc.tensor.matmul(to, rels[:, part, f * 128:(f + 1) * 128], cts[:, g * WIN:(g + 1) * WIN],
                                               start=False, stop=(part == PARTS - 1))
                return ins

            def relation_counts(k):
                for g in range(STEP_G):
                    to = P[0][0:R, 256 + g * WIN:256 + (g + 1) * WIN]
                    for j in range(GC):
                        ins = nc.tensor.matmul(to, onetype[:, k, g * GC + j, :], onehot[:, k, g * GC + j, :],
                                               start=(j == 0), stop=(j == GC - 1))
                return ins

            def sums(a, k):
                pe.wait_ge(cts_ready, a + 1)
                for g in range(STEP_G):
                    r = k % RING_S
                    fills = (a // RING_S + 1) if isinstance(a, int) else None
                    if fills is None:
                        pe.wait_ge(gathered[r * STEP_G + g], (a - k) * (16 * GC // RING_S) + 16 * GC * (k // RING_S + 1))
                    else:
                        pe.wait_ge(gathered[r * STEP_G + g], 16 * GC * fills)
                    if g == 0:
                        pe.wait_ge(acc_added, a * STEP_G)
                    products(r, k % 2, g).then_inc(agg_done, 1)

            def next_counts(a, k):
                if not (isinstance(a, int) and a == STEPS - 1):
                    pe.wait_ge(onehots, a + 2)
                    pe.wait_ge(acc_added, a * STEP_G + 1)
                    relation_counts((k + 1) % 2).then_inc(counts_done, 1)

            def step(a, k):
                sums(a, k)
                next_counts(a, k)

            def transpose_h(t, before):
                pe.wait_ge(h_loaded, t * 16 + 16)
                before()
                for k in range(KT):
                    for j in range(2):
                        at = k * T + j * SUB
                        for part in range(PARTS):
                            ins = nc.tensor.matmul(P[5][:, at:at + SUB], h_in[:, j, part * D + k * 128:part * D + (k + 1) * 128],
                                                   ident16[0:SUB, 0:SUB], start=(part == 0), stop=(part == PARTS - 1))
                ins.then_inc(h_trans, 1)

            def gate(t, row, which):
                nb = t * (-T) + (N - T)
                for m in range(KT):
                    to = P[5][:, m * T:(m + 1) * T]
                    ops = [(w, k) for w in which for k in range(KT)]
                    for n, (w, k) in enumerate(ops):
                        rhs = hT[:, k, :] if w == "h" else acc[:, k, ds(nb, T)]
                        wt = whhT if w == "h" else wihT
                        ins = nc.tensor.matmul(to, wt[:, k, row + m * 128:row + (m + 1) * 128], rhs,
                                               start=(n == 0), stop=(n == len(ops) - 1))
                return ins

            def gate_hn(t):
                pe.wait_ge(hT_ready, t + 1)
                gate(t, 2 * D, "h").then_inc(hn_done, 1)

            def gate_r(t, steps):
                if steps is not None:
                    pe.wait_ge(acc_added, steps * STEP_G)
                pe.wait_ge(hn_ready, t + 1)
                gate(t, 0, "hx").then_inc(r_done, 1)

            def gate_z(t):
                pe.wait_ge(r_ready, t + 1)
                gate(t, D, "hx").then_inc(z_done, 1)

            def gate_in(t):
                pe.wait_ge(z_ready, t + 1)
                gate(t, 2 * D, "x").then_inc(in_done, 1)

            def transpose_gru(t):
                pe.wait_ge(gru_ready, t + 1)
                for j in range(2):
                    for k in range(KT):
                        at = j * D + k * 128
                        ins = nc.tensor.transpose(P[5][0:SUB, at:at + 128], oT[:, k, j * SUB:(j + 1) * SUB], ident[:, :])
                ins.then_inc(gru_trans, 1)

            def transpose_x2(t):
                pe.wait_ge(x2n_ready, t + 1)
                for k in range(KT):
                    for j in range(2):
                        at = k * T + j * SUB
                        ins = nc.tensor.transpose(P[5][:, at:at + SUB], x2n[:, j, k * 128:(k + 1) * 128], ident[0:SUB, 0:SUB])
                ins.then_inc(x2_trans, 1)

            in_steps = [True]

            def first_tile(run):
                transpose_h(0, lambda: None)
                gate_hn(0)
                gate_r(0, FIRST_READ if in_steps[0] else None)
                gate_z(0)
                run(step, 0)
                gate_in(0)
                run(step, 1)
                transpose_gru(0)
                transpose_x2(0)
                pe.wait_ge(s_experts, 16 * 2)

            def tile(i, run, more):
                pe.wait_ge(x2T_ready, i + 1)
                for j in range(2):
                    for k in range(KT):
                        ins = nc.tensor.matmul(P[5][0:SUB, j * NE:(j + 1) * NE], x2T[:, k, j * SUB:(j + 1) * SUB],
                                               wg[:, k, :], start=(k == 0), stop=(k == KT - 1))
                ins.then_inc(scores_done, 1)

                def layer1(e):
                    for s in range(HS):
                        p = e * (HS // 2) + s // 2
                        if s % 2 == 0:
                            pe.wait_ge(gelu_done, i * PAIRS + (p - 2) if p >= 3 else i * PAIRS)
                        to = P[2 + p % 3][:, (s % 2) * T:(s % 2 + 1) * T]
                        for k in range(KT):
                            ins = nc.tensor.matmul(to, w1[:, e, k, s * 128:(s + 1) * 128], x2T[:, k, :],
                                                   start=(k == 0), stop=(k == KT - 1))
                        if s % 2:
                            ins.then_inc(l1_done, 1)

                def layer2(e):
                    pe.wait_ge(moe_added, i * NE + (e - 1) if e >= 2 else i * NE)
                    pe.wait_ge(gelu_done, i * PAIRS + (e + 1) * (HS // 2))
                    for j in range(2):
                        to = P[7 - e % 2][0:SUB, j * D:(j + 1) * D]
                        for s in range(HS):
                            ins = nc.tensor.matmul(to, gT[:, e % 2, s, j * SUB:(j + 1) * SUB], w2[:, e, s, :],
                                                   start=(s == 0), stop=(s == HS - 1))
                    ins.then_inc(l2_done, 1)

                layer1(0)
                pe.wait_ge(mask_ready, i + 1)
                for j in range(2):
                    ins = nc.tensor.transpose(P[5][0:NE, 64 + j * SUB:64 + (j + 1) * SUB], mask[:, j, :], ident[0:SUB, 0:SUB])
                ins.then_inc(mask_trans, 1)
                layer1(1)
                run(sums, 0)
                layer2(0)
                pe.wait_ge(maskT_ready, i + 1)
                for j in range(2):
                    ins = nc.tensor.matmul(P[5][0:SUB, j * D:(j + 1) * D], maskT[:, j * SUB:(j + 1) * SUB], b2s[:, :],
                                           start=True, stop=True)
                ins.then_inc(b2_done, 1)
                run(next_counts, 0)
                for e in range(1, NE):
                    if e + 1 < NE:
                        layer1(e + 1)
                    if more and e == 4:
                        gate_r(i + 1, i * SLOTS + (FIRST + READ_AT) if in_steps[0] else None)
                    if more and e == 5:
                        gate_in(i + 1)
                    if more and e == 6:
                        transpose_gru(i + 1)
                    run(sums, e)
                    if more and e == 1:
                        transpose_h(i + 1, lambda: pe.wait_ge(y_ready, i + 1))
                    if more and e == 2:
                        gate_hn(i + 1)
                    if more and e == 7:
                        transpose_x2(i + 1)
                    layer2(e)
                    run(next_counts, e)
                    if more and e == 4:
                        gate_z(i + 1)

            def fast():
                pe.wait_ge(onehots, 1)
                relation_counts(0).then_inc(counts_done, 1)
                tile_loop(pe, step, first_tile, tile)

            def general():
                in_steps[0] = False
                with pe.Fori(0, STEPS // RING_S) as q:
                    for r in range(RING_S):
                        for g in range(STEP_G):
                            pe.wait_ge(gathered[r * STEP_G + g], q * (16 * GC) + 16 * GC)
                        s = q * RING_S + r
                        pe.wait_ge(g_type, s + 1)
                        pe.nop(nofuse=True)
                        with pe.Fori(0, PADW) as w:
                            v = s * PADW + w
                            pe.wait_ge(g_onehot, v + 1)
                            pe.wait_ge(g_added, v)
                            relation_counts(0).then_inc(g_counts, 1)
                            pe.wait_ge(g_cts, v + 1)
                            products(r, 0, 0)
                            products(r, 0, 1).then_inc(g_agg, 1)
                pe.wait_ge(g_added, STEPS * PADW)
                only_tiles(pe, first_tile, tile)

            paths(pe, fast, general)


_INS = ["x", "src", "dst", "edge_type_16", "L0_gnn_relvectors", "L0_gnn_w_ih", "L0_gnn_w_hh", "L0_gnn_b_ih",
        "L0_gnn_b_hh", "L0_ffn_Wg", "L0_ffn_bg", "L0_ffn_W1", "L0_ffn_b1", "L0_ffn_W2", "L0_ffn_b2"]


def kernel(**inputs):
    import numpy as _np
    import concourse.bacc as _bacc
    from concourse import mybir as _mybir
    from concourse.bass_utils import run_bass_kernel_spmd as _run

    nc = _bacc.Bacc("TRN2", target_bir_lowering=False, num_devices=1)
    arrays, args = {}, []
    named = [(n, _np.ascontiguousarray(inputs[n])) for n in _INS]
    named += list(zip(("c_ident", "c_ramp", "c_limit"), shape_constants()))
    for name, a in named:
        arrays[f"in_{name}_dram"] = a
        args.append(nc.dram_tensor(f"in_{name}_dram", a.shape, _mybir.dt.from_np(a.dtype), kind="ExternalInput").ap())
    out = nc.dram_tensor("out_0_dram", (N, D), _mybir.dt.float32, kind="ExternalOutput").ap()
    gnn_ffn_kernel(nc, *args, out)
    r = _run(nc, [arrays], core_ids=[0])
    return r.results[0]["out_0_dram"]
```

```python
from contextlib import ExitStack

import numpy as np
import concourse.bass as bass
from concourse import mybir

F32 = mybir.dt.float32
BF16 = mybir.dt.bfloat16
F16 = mybir.dt.float16
F32R = mybir.dt.float32r
I32 = mybir.dt.int32
I16 = mybir.dt.int16
U8 = mybir.dt.uint8
U32 = mybir.dt.uint32
ALU = mybir.AluOpType
ACT = mybir.ActivationFunctionType
AX = mybir.AxisListType.X
ds = bass.ds

N, D, E, R = 6250, 256, 200000, 16
NE, H = 8, 512
KT = D // 128
HS = H // 128
EPS = 1e-5

CH = 128
GC = 4
GE = GC * CH
WIN = 48
STEP_G = 2
SC = STEP_G * GC
STEPS = -(-E // (STEP_G * GE))
GROUPS = STEPS * STEP_G
RT = -(-GROUPS // 128)
PARTS = 3
PD = PARTS * D
RING_S = 2
RING_G = RING_S * STEP_G
IDXR = 8
LEAD = 4
NE3 = 3 * NE
R3 = 3 * R

SUB = 125
T = 2 * SUB
TILES = N // T
FIRST = 6
SLOTS = 8
READ_AT = 4
FIRST_READ = 5
LOOPED = (STEPS - FIRST) // SLOTS
LAST_SLOTS = (STEPS - FIRST) % SLOTS
LN_ROWS = N // 128
LN_J = 8
PAIRS = NE * H // 256
LN_CH = LN_ROWS // LN_J
LN_REST = N - 128 * LN_ROWS
XB = 4
BY_ACT = 4
W1_CUTS = 4
HB = 3
BIG = 1.0e6
LIVE = 8 * T
OVER = LIVE
ZEROS = LIVE + WIN
ACOLS = LIVE + 2 * WIN
BANDS = 5
BT = TILES // BANDS
BW = -(-BT * T // WIN)
assert N % T == 0 and LN_ROWS % LN_J == 0 and FIRST % 2 == 0 and SLOTS % IDXR == 0
assert (STEPS - RING_S * 2) % SLOTS == 0 and STEPS % RING_S == 0 and SLOTS % (2 * RING_S) == 0
assert TILES == BANDS * BT and BW * WIN <= OVER
assert LOOPED == TILES - 2 and READ_AT <= LAST_SLOTS


def shape_constants():
    ident = np.eye(128, dtype=np.float32)
    ramp = np.tile(np.concatenate([np.arange(WIN), np.arange(R3) % R]).astype(np.float32), (128, 1))
    g = np.arange(RT * 128)
    a = STEPS - 1 - np.minimum(g // STEP_G, STEPS - 1)
    reads = np.array([FIRST_READ] + [FIRST + SLOTS * i + READ_AT for i in range(TILES - 2)] + [STEPS])
    begun = (reads[None, :] <= a[:, None]).sum(1)
    limit = (N - T * begun).reshape(RT, 128).T
    low = np.maximum(limit - LIVE, 0)
    part = [np.arange(128)[:, None] // rows == np.arange(PARTS)[None, :] for rows in (R, NE)]
    cols = np.concatenate([limit, low] + part, axis=1).astype(np.float32)
    t = np.arange(TILES)
    at = T * ((TILES - 1 - t) % (LIVE // T))
    band_at = T * (BT - 1 - t % BT)
    where = np.concatenate([at, np.where(at == 0, OVER, ZEROS), band_at, np.full(TILES, ZEROS)]).astype(np.int32)[None, :]
    return ident, ramp, np.ascontiguousarray(cols), where


def gnn_ffn_kernel(nc, x, src, dst, etype, rel, w_ih, w_hh, b_ih, b_hh, Wg, bg, W1, b1, W2, b2,
                   c_ident, c_ramp, c_cols, c_where, out):
    h_dram = nc.dram_tensor("h_table", [N, PD], BF16).ap()
    x_rows = x[0:128 * LN_ROWS, :].rearrange("(p j) d -> p j d", p=128)
    h_rows = h_dram[0:128 * LN_ROWS, :].rearrange("(p j) d -> p j d", p=128)

    with ExitStack() as ctx:
        def sb(name, shape, dt=F32):
            return ctx.enter_context(nc.sbuf_tensor(name, shape, dt))

        def sem(name):
            return ctx.enter_context(nc.semaphore(name))

        ident = sb("ident", [128, 128])
        ident16 = sb("ident16", [128, 128], BF16)
        ramp = sb("ramp", [128, WIN + R3])
        cols = sb("cols", [128, 2 * RT + 2 * PARTS])
        limit, low = cols[:, 0:RT], cols[:, RT:2 * RT]
        rel_part, bias_part = cols[:, 2 * RT:2 * RT + PARTS], cols[:, 2 * RT + PARTS:2 * RT + 2 * PARTS]
        where = sb("where", [1, 4 * TILES], I32)
        with nc.sbuf_tensor("stage", [128, 2 * NE * KT * H], F32) as stage:
            pass
        w1h = sb("w1h", [128, NE, KT, H], F32R)
        w1l = sb("w1l", [128, NE, KT, H], F32R)
        w2 = sb("w2", [128, NE, HS, D])
        wih_h = sb("wih_h", [128, KT, 3 * D], F32R)
        wih_l = sb("wih_l", [128, KT, 3 * D], F32R)
        whh_h = sb("whh_h", [128, KT, 3 * D], F32R)
        whh_l = sb("whh_l", [128, KT, 3 * D], F32R)
        rels = sb("rels", [R3, D], BF16)
        wg = sb("wg", [128, KT, NE])
        wghl = sb("wghl", [128, KT, 2, NE], F32R)
        bgb = sb("bgb", [128, 2 * NE])
        b2s = sb("b2s", [NE3, D], BF16)
        bias = sb("bias", [128, 44])
        half_rz = sb("half_rz", [128, 4])
        b1c = bias[:, 0:32].rearrange("p (e s) -> p e s", e=NE)
        bihc = bias[:, 32:38]
        bhhc = bias[:, 38:44]
        src_t = sb("src_t", [128, GROUPS * GC], I16)
        dst_t = sb("dst_t", [128, GROUPS * GC], I16)
        typ_t = sb("typ_t", [128, GROUPS * GC], U8)
        base_i = sb("base_i", [1, GROUPS], I32)
        gmax = sb("gmax", [128, RT])
        gmin = sb("gmin", [128, RT])
        base = sb("base", [128, RT])
        viol = sb("viol", [128, 3, RT])
        vsum = sb("vsum", [128, 1])
        ok = sb("ok", [128, 1])
        flag = sb("flag", [1, 1], I32)
        acc = sb("acc", [128, KT, ACOLS])
        ring = sb("ring", [128, RING_G, GC, PD], BF16)
        idx = sb("idx", [128, IDXR, SC], I32)
        onehot = sb("onehot", [128, 2, SC, WIN], BF16)
        onetype = sb("onetype", [128, 2, SC, R3], BF16)
        cts = sb("cts", [R3, STEP_G * WIN], F16)
        ramp_w = sb("ramp_w", [128, WIN])
        h_h = sb("h_h", [128, KT, T], F32R)
        h_l = sb("h_l", [128, KT, T], F32R)
        x1 = sb("x1", [SUB, 2, D])
        x2h = sb("x2h", [128, KT, T], F32R)
        x2l = sb("x2l", [128, KT, T], F32R)
        red_h = sb("red_h", [128, KT, T], F32R)
        red_l = sb("red_l", [128, KT, T], F32R)
        zero = sb("zero", [128, 1])
        gT = sb("gT", [128, 2, HS, T])
        rz = sb("rz", [128, 2, KT * D])
        rT = rz[:, 0, 0:KT * T].rearrange("p (k t) -> p k t", k=KT)
        zT = rz[:, 1, 0:KT * T].rearrange("p (k t) -> p k t", k=KT)
        x2n = rz[0:SUB, 1, :].rearrange("p (j d) -> p j d", j=2)
        rz16 = rz[:, :, :].rearrange("p a d -> p (a d)").bitcast(BF16)
        h_in = rz16[0:SUB, 0:2 * PD].rearrange("p (j d) -> p j d", j=2)
        oT = sb("oT", [128, KT, T])
        y = sb("y", [SUB, 2, D])
        scores = sb("scores", [SUB, 2, NE])
        top = sb("top", [SUB, 2, 8])
        topi = sb("topi", [SUB, 2, 8], U32)
        topf = sb("topf", [SUB, 2, 8])
        mask = sb("mask", [SUB, 2, PARTS, NE])
        mask1 = sb("mask1", [SUB, 2, NE])
        maskT = sb("maskT", [NE3, T], BF16)
        st = sb("st", [128, LN_J, 6])
        mv = sb("mv", [128, 2, LN_J, 2])
        var = sb("var", [128, 2, LN_J])
        std = sb("std", [128, 2, LN_J])
        rstd = sb("rstd", [128, 2, LN_J])
        nmr = sb("nmr", [128, 2, LN_J])
        xc = stage[:, 0:XB * LN_J * D].rearrange("p (c j d) -> p c j d", c=XB, j=LN_J)
        o = XB * LN_J * D
        nat = stage[:, o:o + 3 * RT * GE].rearrange("p (s r e) -> p s r e", s=3, r=RT)
        nat_i = nat.bitcast(I32)
        o += 3 * RT * GE
        tmin = stage[:, o:o + GE]
        o += GE
        ones = stage[:, o:o + 128]
        bias_rows = stage[0:44, o + 128:o + 256]
        assert o + 256 <= 2 * NE * KT * H
        raw1 = w2[:, :, :, :].rearrange("p e s d -> p (e s d)").rearrange("p (e k h) -> p e k h", e=NE, k=KT)
        flat = acc[:, :, :].rearrange("p k n -> p (k n)")
        wnat = flat[:, 0:2 * 6 * D].rearrange("p (w m d) -> p w m d", w=2, m=6)
        w2f = w2[:, :, :, :].rearrange("p e s d -> p (e s d)").bitcast(BF16)
        res = w2f[:, 0:2 * 2 * LN_J * D].bitcast(F32).rearrange("p (c j d) -> p c j d", c=2, j=LN_J)
        hc = [w2f[:, 4 * LN_J * D:4 * LN_J * D + LN_J * PD].rearrange("p (j q) -> p j q", j=LN_J)]
        ringf = ring[:, :, :, :].rearrange("p g c q -> p (g c q)")
        hc += [ringf[:, c * LN_J * PD:(c + 1) * LN_J * PD].rearrange("p (j q) -> p j q", j=LN_J) for c in range(2)]
        gflat = gT[:, :, :, :].rearrange("p b s t -> p (b s t)")
        diag = gflat[:, 0:RT * 128]
        base_bc = gflat[:, RT * 128:2 * RT * 128]
        rel_rest = gflat[0:R3, 2 * RT * 128:2 * RT * 128 + D]
        rel_sum = gflat[0:R3, 2 * RT * 128 + D:2 * RT * 128 + 2 * D]
        turn = gflat[0:1, 3 * RT * 128:3 * RT * 128 + GROUPS]
        raw_rel = y[0:R3, 0, :]
        raw_b2 = oT[:, :, :].rearrange("p k t -> p (k t)")[0:NE3, 0:D]

        P = [ctx.enter_context(nc.psum_tensor(f"P{b}", [128, 512], F32)) for b in range(8)]

        s_const = sem("s_const")
        s_ones = sem("s_ones")
        s_pads = sem("s_pads")
        s_nat = [sem(f"s_nat{n}") for n in range(3)]
        s_wnat = sem("s_wnat")
        s_weights = sem("s_weights")
        s_experts = sem("s_experts")
        s_xc = [sem(f"s_xc{c}") for c in range(XB)]
        s_hst = [sem(f"s_hst{c}") for c in range(HB)]
        s_ln_var = sem("s_ln_var")
        s_ln_std = sem("s_ln_std")
        s_ln_coef = sem("s_ln_coef")
        s_ln_h = sem("s_ln_h")
        s_part1 = sem("s_part1")
        s_rest1 = sem("s_rest1")
        s_part2 = sem("s_part2")
        s_part3 = sem("s_part3")
        s_natf = sem("s_natf")
        s_viol = sem("s_viol")
        s_violb = sem("s_violb")
        s_diag = sem("s_diag")
        s_baseb = sem("s_baseb")
        s_based = sem("s_based")
        s_tr = sem("s_tr")
        s_dst_out = sem("s_dst_out")
        s_tr_out = sem("s_tr_out")
        w1_high = sem("w1_high")
        w1_low = sem("w1_low")
        s_raw1 = sem("s_raw1")
        s_flag = sem("s_flag")
        s_bias = sem("s_bias")
        s_zero = sem("s_zero")
        s_small = sem("s_small")
        gathered = [sem(f"gathered{r}") for r in range(RING_G)]
        idx_ready = sem("idx_ready")
        onehots = sem("onehots")
        counts_done = sem("counts_done")
        cts_ready = sem("cts_ready")
        agg_done = sem("agg_done")
        acc_added = sem("acc_added")
        g_idx = sem("g_idx")
        g_type = sem("g_type")
        g_onehot = sem("g_onehot")
        g_counts = sem("g_counts")
        g_cts = sem("g_cts")
        g_agg = sem("g_agg")
        g_half = sem("g_half")
        g_added = sem("g_added")
        g_ramp = sem("g_ramp")
        h_loaded = sem("h_loaded")
        x_loaded = sem("x_loaded")
        h_trans = sem("h_trans")
        hT_ready = sem("hT_ready")
        h_l_ready = sem("h_l_ready")
        red_ready = sem("red_ready")
        hn_done = sem("hn_done")
        hn_ready = sem("hn_ready")
        r_done = sem("r_done")
        r_ready = sem("r_ready")
        rhn_ready = sem("rhn_ready")
        z_done = sem("z_done")
        z_ready = sem("z_ready")
        in_done = sem("in_done")
        pre_n = sem("pre_n")
        n_ready = sem("n_ready")
        gru_ready = sem("gru_ready")
        gru_trans = sem("gru_trans")
        x1_ready = sem("x1_ready")
        var_ready = sem("var_ready")
        std_ready = sem("std_ready")
        x2n_ready = sem("x2n_ready")
        x2_trans = sem("x2_trans")
        x2h_ready = sem("x2h_ready")
        x2l_ready = sem("x2l_ready")
        scores_done = sem("scores_done")
        mask_ready = sem("mask_ready")
        mask_trans = sem("mask_trans")
        maskT_ready = sem("maskT_ready")
        b2_done = sem("b2_done")
        y_ready = sem("y_ready")
        l1_done = sem("l1_done")
        gelu_done = sem("gelu_done")
        l2_done = sem("l2_done")
        moe_added = sem("moe_added")
        y_moved = sem("y_moved")
        dve_chain = sem("dve_chain")

        def table_whole(eng):
            for r in range(HB):
                eng.wait_ge(s_hst[r], 16 * len(range(r, LN_CH + 1, HB)))

        def chunk_rows(c):
            return (128, LN_J) if c < LN_CH else (LN_REST, 1)

        def paths(eng, fast, general):
            eng.wait_ge(s_flag, 1)
            bad = eng.value_load(flag[0:1, 0:1], min_val=0, max_val=2 * RT * 128)
            with eng.If(bad < 1):
                fast()
            with eng.Else():
                general()
            eng.end_ifs()

        def no_steps(f, k):
            return None

        def bank(gate, alone):
            return P[{"hn": 2, "r": 3, "in": 4, "z": 5}[gate] if alone else 5]

        def tile_loop(eng, step, first_h, first_tile, tile, between=None):
            for a in range(FIRST_READ):
                step(a, a)
                if a == 1:
                    first_h(0)
                if between:
                    for c in {2: (0, 1), 3: (2,)}.get(a, ()):
                        between(c)
            first_tile(0, lambda f, k: f(FIRST_READ + k, FIRST_READ + k) if FIRST_READ + k < FIRST else None)
            with eng.Fori(0, LOOPED) as i:
                tile(i, lambda f, k: f(i * SLOTS + (FIRST + k), FIRST + k), True)
            i = LOOPED
            tile(i, lambda f, k: f(i * SLOTS + FIRST + k, FIRST + k) if k < READ_AT else None, True,
                 range(READ_AT, LAST_SLOTS))
            tile(i + 1, no_steps, False)

        def by_bands(eng, sum_band, gru_h, gru, tile):
            with eng.Fori(0, BANDS) as b:
                sum_band(b)
                with eng.Fori(0, BT) as j:
                    t = b * BT + j
                    gru_h(t)
                    gru(t, no_steps)
                    tile(t, no_steps, False)

        block = ctx.enter_context(nc.Block())

        @block.sync
        def _(sp):
            def load_chunk(c):
                if c < LN_CH:
                    sp.dma_start(xc[:, c % XB, :, :], x_rows[:, c * LN_J:(c + 1) * LN_J, :]).then_inc(s_xc[c % XB], 16)
                else:
                    sp.dma_start(xc[0:LN_REST, c % XB, 0, :], x[128 * LN_ROWS:N, :]).then_inc(s_xc[c % XB], 16)

            load_chunk(0)
            load_chunk(1)
            for to, a in ((ident, c_ident), (ramp, c_ramp), (cols, c_cols), (where, c_where)):
                sp.dma_start(to[:, :], a).then_inc(s_const, 16)
            rows = RT - 1
            whole = E // GE - rows * 128
            left = E - (rows * 128 + whole) * GE
            for n, a in enumerate((dst, src, etype)):
                sp.dma_start(nat_i[:, n, 0:rows, :],
                             a[0:rows * 128 * GE].rearrange("(r p e) -> p r e", p=128, e=GE)).then_inc(s_nat[n], 16)
                if n == 0:
                    sp.wait_ge(s_pads, 1)
                at = rows * 128 * GE
                sp.dma_start(nat_i[0:whole, n, rows, :],
                             a[at:at + whole * GE].rearrange("(p e) -> p e", e=GE)).then_inc(s_nat[n], 16)
                at += whole * GE
                sp.dma_start(nat_i[whole:whole + 1, n, rows, 0:left],
                             a[at:at + left].rearrange("(p e) -> p e", p=1)).then_inc(s_nat[n], 16)
                if n < 2:
                    load_chunk(n + 2)
            for n, w in enumerate((w_ih, w_hh)):
                sp.dma_start(wnat[:, n, :, :], w.rearrange("(m p) d -> p m d", p=128)).then_inc(s_wnat, 16)
            sp.dma_start(bias_rows[0:32, :], b1.rearrange("e (s p) -> (e s) p", p=128)).then_inc(s_wnat, 16)
            sp.dma_start(bias_rows[32:38, :], b_ih.rearrange("(m p) -> m p", p=128)).then_inc(s_wnat, 16)
            sp.dma_start(bias_rows[38:44, :], b_hh.rearrange("(m p) -> m p", p=128)).then_inc(s_wnat, 16)
            for part in range(PARTS):
                sp.dma_start(y[part * R:(part + 1) * R, 0, :], rel).then_inc(y_moved, 16)
            sp.dma_start(wg[:, :, :], Wg.rearrange("(k p) e -> p k e", p=128)).then_inc(s_weights, 16)
            for j in range(2):
                sp.dma_start(bgb[:, j * NE:(j + 1) * NE], bg.rearrange("(a e) -> a e", a=1).to_broadcast([128, NE])).then_inc(s_weights, 16)
            for part in range(PARTS):
                sp.dma_start(raw_b2[part * NE:(part + 1) * NE, :], b2).then_inc(s_weights, 16)
            for c in range(LN_CH + 1):
                np_, nj = chunk_rows(c)
                if c + XB <= LN_CH:
                    sp.wait_ge(s_rest1, c + 1)
                    load_chunk(c + XB)
                sp.wait_ge(s_part3, c + 1)
                if c < LN_CH:
                    sp.dma_start(h_rows[:, c * LN_J:(c + 1) * LN_J, :], hc[c % HB]).then_inc(s_hst[c % HB], 16)
                else:
                    sp.dma_start(h_dram[128 * LN_ROWS:N, :], hc[c % HB][0:LN_REST, 0, :]).then_inc(s_hst[c % HB], 16)
            table_whole(sp)

            def node_rows(t, i):
                return t[ds(i * (-T) + (N - T), T), :].rearrange("(j p) d -> p j d", p=SUB)

            sp.dma_start(h_in[:, :, :], node_rows(h_dram, 0)).then_inc(h_loaded, 16)
            sp.dma_start(x1[:, :, :], node_rows(x, 0)).then_inc(x_loaded, 16)
            sp.dma_start(raw1, W1.rearrange("e (k p) h -> p e k h", p=128)).then_inc(s_raw1, 16)
            for c in range(W1_CUTS):
                sp.wait_ge(w1_low, c + 1)
                piece = slice(c * NE // W1_CUTS, (c + 1) * NE // W1_CUTS)
                sp.dma_start(w2[:, piece, :, :], W2[piece, :, :].rearrange("e (s p) d -> p e s d", p=128)).then_inc(s_experts, 16)
            with sp.Fori(0, TILES - 1) as i:
                sp.wait_ge(x2_trans, i + 1)
                sp.dma_start(h_in[:, :, :], node_rows(h_dram, i + 1)).then_inc(h_loaded, 16)
                sp.wait_ge(y_ready, i + 1)
                sp.dma_start(x1[:, :, :], node_rows(x, i + 1)).then_inc(x_loaded, 16)
                sp.wait_ge(moe_added, i * NE + NE)
                sp.dma_start(node_rows(out, i), y[:, :, :]).then_inc(y_moved, 16)
            sp.wait_ge(moe_added, TILES * NE)
            sp.dma_start(node_rows(out, TILES - 1), y[:, :, :]).then_inc(y_moved, 16)
            sp.wait_ge(y_moved, 16 * (3 + TILES))

        @block.gpsimd
        def _(pool):
            nc.gpsimd.memset(ones[:, :], 1.0).then_inc(s_ones, 1)
            for c in range(LN_CH + 1):
                np_, nj = chunk_rows(c)
                pool.wait_ge(s_part1, c + 1)
                if c >= 2:
                    pool.wait_ge(s_part3, c - 1)
                nc.gpsimd.tensor_tensor(res[0:np_, c % 2, 0:nj, :], xc[0:np_, c % XB, 0:nj, :],
                                        hc[c % HB][0:np_, 0:nj, 0:D], ALU.subtract).then_inc(s_rest1, 1)
                if c < 2:
                    pool.wait_ge(s_nat[c + 1], 16 * 3)
                    nc.gpsimd.tensor_copy(nat[:, c + 1, :, :], nat_i[:, c + 1, :, :]).then_inc(s_natf, 1)
            pool.wait_ge(s_tr, 3 * RT + 6)
            nc.gpsimd.memset(acc[:, :, :], 0.0).then_inc(s_zero, 1)
            table_whole(pool)

            def gather(r, slot, g):
                for j in range(GC):
                    nc.gpsimd.indirect_dma_start(
                        out=ring[:, r, j, :], out_offset=None, in_=h_dram,
                        in_offset=bass.IndirectOffsetOnAxis(ap=idx[:, slot, g * GC + j:g * GC + j + 1], axis=0),
                    ).then_inc(gathered[r], 16)

            def fast():
                for a in range(2 * RING_S):
                    pool.wait_ge(idx_ready, a + 1)
                    for g in range(STEP_G):
                        n = a * STEP_G + g
                        if n >= RING_G:
                            pool.wait_ge(agg_done, n - RING_G + 1)
                        gather(n % RING_G, a, g)
                with pool.Fori(0, (STEPS - 2 * RING_S) // SLOTS) as q:
                    for k in range(SLOTS):
                        pool.wait_ge(idx_ready, q * SLOTS + (2 * RING_S + k + 1))
                        for g in range(STEP_G):
                            n = (2 * RING_S + k) * STEP_G + g
                            pool.wait_ge(agg_done, q * (SLOTS * STEP_G) + (n - RING_G + 1))
                            pool.nop(nofuse=True)
                            gather(n % RING_G, (2 * RING_S + k) % IDXR, g)

            def general():
                with pool.Fori(0, BANDS * (STEPS // RING_S)) as q:
                    pool.wait_ge(g_idx, q + 1)
                    pool.nop(nofuse=True)
                    for r in range(RING_S):
                        for g in range(STEP_G):
                            gather(r * STEP_G + g, r, g)

            paths(pool, fast, general)

        @block.scalar
        def _(act):
            outs = []

            def part2(c):
                np_, nj = chunk_rows(c)
                act.wait_ge(s_rest1, c + 1)
                nc.scalar.activation(hc[c % HB][0:np_, 0:nj, D:2 * D], res[0:np_, c % 2, 0:nj, :], ACT.Copy).then_inc(s_part2, 1)

            def out_table(q):
                n, r = divmod(q, RT)
                g = min(128, GROUPS - r * 128)
                act.wait_ge(s_tr, q + 1)
                o = (dst_t, src_t, typ_t)[n][:, r * 128 * GC:(r * 128 + g) * GC].rearrange("p (g j) -> p g j", j=GC)
                nc.scalar.activation(o, P[2 + q % 4][:, :].rearrange("p (j g) -> p g j", j=GC)[:, 0:g, :], ACT.Copy).then_inc(s_tr_out, 1)

            def out_weights(q):
                act.wait_ge(s_tr, 3 * RT + q + 1)
                w, m = (wih_h, whh_h)[q // 3], q % 3
                nc.scalar.activation(w[:, :, m * 256:(m + 1) * 256],
                                     P[(6, 7, 2, 3, 4, 5)[q]][:, :].rearrange("p (k m) -> p k m", k=KT), ACT.Copy).then_inc(s_tr_out, 1)

            def roots(c):
                np_, nj = chunk_rows(c)
                act.wait_ge(s_ln_var, c + 1)
                nc.scalar.activation(std[0:np_, c % 2, 0:nj], var[0:np_, c % 2, 0:nj], ACT.Sqrt).then_inc(s_ln_std, 1)

            roots(0)
            for c in range(LN_CH + 1):
                np_, nj = chunk_rows(c)
                if c < LN_CH:
                    roots(c + 1)
                act.wait_ge(s_ln_coef, c + 1)
                for j in range(nj):
                    ins = nc.scalar.activation(xc[0:np_, c % XB, j, :], xc[0:np_, c % XB, j, :], ACT.Identity,
                                               bias=nmr[0:np_, c % 2, j:j + 1], scale=rstd[0:np_, c % 2, j:j + 1])
                ins.then_inc(s_ln_h, 1)
                act.wait_ge(s_ln_h, c + 1)
                if c >= HB:
                    act.wait_ge(s_hst[c % HB], 16 * (c // HB))
                nc.scalar.activation(hc[c % HB][0:np_, 0:nj, 0:D], xc[0:np_, c % XB, 0:nj, :], ACT.Copy).then_inc(s_part1, 1)
                if 0 < c <= BY_ACT:
                    part2(c - 1)
                if c in (3, 4):
                    for r in range(RT):
                        out_table((c - 2) * RT + r)
            for q in range(6):
                out_weights(q)

            def step(a, k):
                if not (isinstance(a, int) and a == STEPS - 1):
                    act.wait_ge(counts_done, a + 2)
                    nc.scalar.activation(cts[:, :], P[0][0:R3, 256:256 + STEP_G * WIN], ACT.Copy).then_inc(cts_ready, 1)

            b5 = P[5][:, 0:KT * T]

            def copy_hT(t):
                act.wait_ge(h_trans, t + 1)
                nc.scalar.activation(h_h[:, :, :].rearrange("p k t -> p (k t)"), b5, ACT.Copy).then_inc(hT_ready, 1)

            def bias_hn(t, alone=False):
                b = bank("hn", alone)
                act.wait_ge(hn_done, t + 1)
                for m in range(KT):
                    ins = nc.scalar.activation(oT[:, m, :], b[:, m * T:(m + 1) * T], ACT.Identity, bias=bhhc[:, 4 + m:5 + m])
                ins.then_inc(hn_ready, 1)

            def gate_r(t, alone=False):
                b = bank("r", alone)
                act.wait_ge(r_done, t + 1)
                for m in range(KT):
                    ins = nc.scalar.activation(rT[:, m, :], b[:, m * T:(m + 1) * T], ACT.Tanh,
                                               bias=half_rz[:, m:m + 1], scale=0.5)
                ins.then_inc(r_ready, 1)

            def gate_z(t, alone=False):
                b = bank("z", alone)
                act.wait_ge(z_done, t + 1)
                for m in range(KT):
                    ins = nc.scalar.activation(zT[:, m, :], b[:, m * T:(m + 1) * T], ACT.Tanh,
                                               bias=half_rz[:, 2 + m:3 + m], scale=0.5)
                ins.then_inc(z_ready, 1)

            def gate_n(t):
                act.wait_ge(pre_n, t + 1)
                for m in range(KT):
                    ins = nc.scalar.activation(rT[:, m, :], oT[:, m, :], ACT.Tanh, bias=bihc[:, 4 + m:5 + m])
                ins.then_inc(n_ready, 1)

            def root(t):
                act.wait_ge(var_ready, t + 1)
                nc.scalar.activation(std[0:SUB, 0, 0:2], var[0:SUB, 0, 0:2], ACT.Sqrt).then_inc(std_ready, 1)

            def high_x2(t):
                act.wait_ge(x2_trans, t + 1)
                nc.scalar.activation(x2h[:, :, :].rearrange("p k t -> p (k t)"), b5, ACT.Copy).then_inc(x2h_ready, 1)

            def gru_h(t):
                copy_hT(t)
                bias_hn(t, True)

            def gru(t, run):
                if run is not no_steps:
                    split_w1(W1_CUTS - 1)
                gate_r(t, True)
                gate_n(t)
                gate_z(t, True)
                root(t)
                run(step, 0)
                high_x2(t)

            def split_w1(c):
                if c == 0:
                    act.wait_ge(s_raw1, 16)
                e = c * NE // W1_CUTS
                nc.scalar.activation(w1h[:, e:e + NE // W1_CUTS, :, :], raw1[:, e:e + NE // W1_CUTS, :, :], ACT.Copy).then_inc(w1_high, 1)

            def tile(i, run, more, extra=()):
                def gelu(e):
                    if e >= 2:
                        act.wait_ge(l2_done, i * NE + (e - 1))
                    for s in range(HS):
                        p = e * (HS // 2) + s // 2
                        if s % 2 == 0:
                            act.wait_ge(l1_done, i * PAIRS + (p + 1))
                        ins = nc.scalar.activation(gT[:, e % 2, s, :], P[2 + p % 3][:, (s % 2) * T:(s % 2 + 1) * T], ACT.Gelu,
                                                   bias=b1c[:, e, s:s + 1])
                        if s % 2:
                            ins.then_inc(gelu_done, 1)

                gelu(0)
                act.wait_ge(mask_trans, i + 1)
                nc.scalar.activation(maskT[:, :], P[5][0:NE3, 64:64 + T], ACT.Copy).then_inc(maskT_ready, 1)
                gelu(1)
                run(step, 0)
                for e in range(1, NE):
                    if e + 1 < NE:
                        gelu(e + 1)
                    if more and e == 1:
                        copy_hT(i + 1)
                    if more and e == 2:
                        bias_hn(i + 1)
                    if more and e == 4:
                        gate_r(i + 1)
                    if more and e == 5:
                        gate_z(i + 1)
                    if more and e == 6:
                        root(i + 1)
                    if more and e == 7:
                        high_x2(i + 1)
                    run(step, e)
                    if e == READ_AT - 1:
                        for k in extra:
                            step(i * SLOTS + FIRST + k, FIRST + k)
                    if more and e == 4:
                        gate_n(i + 1)

            def fast():
                act.wait_ge(s_small, 1)
                act.wait_ge(counts_done, 1)
                nc.scalar.activation(cts[:, :], P[0][0:R3, 256:256 + STEP_G * WIN], ACT.Copy).then_inc(cts_ready, 1)
                tile_loop(act, step, gru_h, gru, tile, split_w1)

            def general():
                act.wait_ge(s_small, 1)
                for c in range(W1_CUTS):
                    split_w1(c)

                def sum_band(b):
                    with act.Fori(0, STEPS * BW) as v:
                        act.wait_ge(g_counts, b * (STEPS * BW) + v + 1)
                        nc.scalar.activation(cts[:, :], P[0][0:R3, 256:256 + STEP_G * WIN], ACT.Copy).then_inc(g_cts, 1)

                by_bands(act, sum_band, gru_h, gru, tile)

            paths(act, fast, general)

        @block.vector
        def _(dve):
            count = [0]

            at = [0]
            LINKS = 15

            def link(ins, alone=False):
                count[0] += 1
                ins.then_inc(dve_chain, 1)
                dve.wait_ge(dve_chain, at[0] * LINKS + count[0])
                if alone:
                    dve.nop(nofuse=True)

            nc.vector.memset(zero[:, :], 0.0)
            nc.vector.memset(nat[:, 1:3, RT - 1, :], 0.0)
            nc.vector.memset(nat_i[:, 0, RT - 1, :], -1).then_inc(s_pads, 1)

            def statistics(c):
                np_, nj = chunk_rows(c)
                b = c % 2
                dve.wait_ge(s_xc[c % XB], 16 * (c // XB + 1))
                for j in range(nj):
                    ins = nc.vector.bn_stats(st[0:np_, j, :], xc[0:np_, c % XB, j, :])
                link(ins)
                for j in range(nj):
                    ins = nc.vector.bn_aggr(mv[0:np_, b, j, :], st[0:np_, j, :])
                link(ins)
                nc.vector.tensor_scalar_add(var[0:np_, b, 0:nj], mv[0:np_, b, 0:nj, 1], EPS).then_inc(s_ln_var, 1)

            def coefficients(c):
                np_, nj = chunk_rows(c)
                b = c % 2
                dve.wait_ge(s_ln_std, c + 1)
                if c >= 2:
                    dve.wait_ge(s_ln_h, c - 1)
                link(nc.vector.reciprocal(rstd[0:np_, b, 0:nj], std[0:np_, b, 0:nj]))
                nc.vector.scalar_tensor_tensor(nmr[0:np_, b, 0:nj], mv[0:np_, b, 0:nj, 0], -1.0, rstd[0:np_, b, 0:nj],
                                               ALU.mult, ALU.mult).then_inc(s_ln_coef, 1)
                dve.wait_ge(s_ln_coef, c + 1)

            def part3(c):
                np_, nj = chunk_rows(c)
                if c < BY_ACT:
                    dve.wait_ge(s_part2, c + 1)
                else:
                    dve.wait_ge(s_rest1, c + 1)
                    link(nc.vector.tensor_copy(hc[c % HB][0:np_, 0:nj, D:2 * D], res[0:np_, c % 2, 0:nj, :]))
                nc.vector.tensor_tensor(hc[c % HB][0:np_, 0:nj, 2 * D:PD], res[0:np_, c % 2, 0:nj, :],
                                        hc[c % HB][0:np_, 0:nj, D:2 * D], ALU.subtract).then_inc(s_part3, 1)

            def edge_windows():
                dve.wait_ge(s_nat[0], 16 * 3)
                link(nc.vector.tensor_copy(nat[:, 0, :, :], nat_i[:, 0, :, :]))
                nc.vector.tensor_reduce(gmax[:, :], nat[:, 0, :, :], AX, ALU.max)
                link(nc.vector.tensor_scalar(tmin[:, :], nat[:, 0, RT - 1, :], 0.0, BIG, ALU.is_lt, ALU.mult))
                link(nc.vector.tensor_tensor(tmin[:, :], tmin[:, :], nat[:, 0, RT - 1, :], ALU.add))
                nc.vector.tensor_reduce(gmin[:, RT - 1:RT], tmin[:, :], AX, ALU.min)
                nc.vector.tensor_reduce(gmin[:, 0:RT - 1], nat[:, 0, 0:RT - 1, :], AX, ALU.min)
                link(nc.vector.tensor_scalar(base[:, :], gmax[:, :], -float(WIN - 1), 0.0, ALU.add, ALU.max))
                dve.wait_ge(s_const, 16 * 4)
                nc.vector.tensor_tensor(viol[:, 0, :], gmin[:, :], base[:, :], ALU.is_lt)
                nc.vector.tensor_tensor(viol[:, 1, :], gmax[:, :], limit, ALU.is_ge)
                link(nc.vector.tensor_scalar(viol[:, 2, :], gmax[:, :], 0.0, None, ALU.is_ge))
                link(nc.vector.tensor_tensor(low, low, viol[:, 2, :], ALU.mult))
                link(nc.vector.tensor_tensor(viol[:, 2, :], base[:, :], low, ALU.is_lt))
                nc.vector.tensor_reduce(vsum[:, :], viol[:, :, :].rearrange("p a b -> p (a b)"), AX, ALU.add).then_inc(s_viol, 1)

            def bases():
                dve.wait_ge(s_violb, 1)
                link(nc.vector.tensor_scalar(ok[:, :], P[0][:, 0:1], 0.5, None, ALU.is_lt))
                link(nc.vector.tensor_scalar(base[:, :], base[:, :], ok[:, 0:1], None, ALU.mult))
                for r in range(RT):
                    ins = nc.vector.tensor_scalar(diag[:, r * 128:(r + 1) * 128], ident[:, :], base[:, r:r + 1], None, ALU.mult)
                ins.then_inc(s_diag, 1)

            def places():
                dve.wait_ge(s_baseb, 1)
                groups = P[1][0:1, 0:GROUPS]
                link(nc.vector.tensor_scalar(turn, groups, float(LIVE), -float(LIVE), ALU.is_ge, ALU.mult))
                link(nc.vector.tensor_tensor(turn, turn, groups, ALU.add))
                for more in range(1, (N - 1) // LIVE):
                    link(nc.vector.tensor_copy(base_i[:, :], turn))
                    link(nc.vector.tensor_scalar(turn, turn, float(LIVE), -float(LIVE), ALU.is_ge, ALU.mult))
                    if more < (N - 1) // LIVE - 1:
                        link(nc.vector.tensor_tensor(turn, turn, base_i[:, :], ALU.add))
                link(nc.vector.tensor_tensor(base_i[:, :], turn, base_i[:, :], ALU.add))
                link(nc.vector.tensor_copy(base_bc[:, :], P[1][:, :]))

            def targets():
                for r in range(RT):
                    g = min(128, GROUPS - r * 128)
                    dve.wait_ge(s_tr, r + 1)
                    nc.vector.tensor_tensor(dst_t[:, r * 128 * GC:(r * 128 + g) * GC].rearrange("p (g j) -> p g j", j=GC),
                                            P[2 + r % 4][:, :].rearrange("p (j g) -> p g j", j=GC)[:, 0:g, :],
                                            base_bc[:, r * 128:r * 128 + g].unsqueeze(2).to_broadcast([128, g, GC]),
                                            ALU.subtract).then_inc(s_dst_out, 1)
                link(nc.vector.tensor_copy(flag[:, :], P[0][0:1, 0:1]))

            def keep_parts(to, raw, rows, is_part):
                rest, kept = rel_rest[0:rows, :], rel_sum[0:rows, :]
                link(nc.vector.tensor_copy(to, raw))
                link(nc.vector.tensor_tensor(rest, raw, to, ALU.subtract))
                link(nc.vector.tensor_scalar(kept, to, is_part[0:rows, 0:1], None, ALU.mult))
                for part in (1, 2):
                    link(nc.vector.tensor_copy(to, rest))
                    link(nc.vector.tensor_tensor(rest, rest, to, ALU.subtract))
                    link(nc.vector.scalar_tensor_tensor(kept, to, is_part[0:rows, part:part + 1], kept, ALU.mult, ALU.add))
                link(nc.vector.tensor_copy(to, kept))

            def small_weights():
                dve.wait_ge(y_moved, 16 * 3)
                keep_parts(rels[:, :], raw_rel, R3, rel_part)
                nc.vector.tensor_copy(ident16[:, :], ident[:, :])
                dve.wait_ge(s_weights, 16 * 6)
                keep_parts(b2s[:, :], raw_b2, NE3, bias_part)
                link(nc.vector.tensor_copy(wghl[:, :, 0, :], wg[:, :, :]))
                link(nc.vector.tensor_tensor(wghl[:, :, 1, :], wg[:, :, :], wghl[:, :, 0, :], ALU.subtract))
                dve.wait_ge(s_tr_out, 2 * RT + 6)
                for q in range(6):
                    (low_w, high_w), m = ((wih_l, wih_h), (whh_l, whh_h))[q // 3], q % 3
                    nc.vector.tensor_tensor(low_w[:, :, m * 256:(m + 1) * 256],
                                            P[(6, 7, 2, 3, 4, 5)[q]][:, :].rearrange("p (k m) -> p k m", k=KT),
                                            high_w[:, :, m * 256:(m + 1) * 256], ALU.subtract)
                dve.wait_ge(s_bias, 1)
                link(nc.vector.tensor_copy(bias[:, :], P[1][:, 0:44]))
                link(nc.vector.tensor_tensor(half_rz[:, :], bihc[:, 0:4], bhhc[:, 0:4], ALU.add))
                nc.vector.tensor_scalar(half_rz[:, :], half_rz[:, :], 0.5, None, ALU.mult).then_inc(s_small, 1)
                dve.wait_ge(s_zero, 1)

            statistics(0)
            statistics(1)
            coefficients(0)
            between = {0: edge_windows, 1: bases, 2: places, 3: targets}
            for c in range(LN_CH + 1):
                if c + 2 <= LN_CH:
                    statistics(c + 2)
                if c + 1 <= LN_CH:
                    coefficients(c + 1)
                if c in between:
                    between[c]()
                if c:
                    part3(c - 1)
            part3(LN_CH)
            dve.wait_ge(s_tr_out, 2 * RT)
            nc.vector.memset(ok[:, :], 0.0).then_inc(s_flag, 1)

            def lay_indices(a, slot):
                col = (a * (-SC) + (STEPS - 1) * SC) if not isinstance(a, int) else (STEPS - 1 - a) * SC
                nc.vector.tensor_copy(idx[:, slot, :], src_t[:, ds(col, SC)]).then_inc(idx_ready, 1)

            def build(a, k):
                col = (a * (-SC) + (STEPS - 1) * SC) if not isinstance(a, int) else (STEPS - 1 - a) * SC
                nc.vector.tensor_tensor(onehot[:, k % 2, :, :],
                                        dst_t[:, ds(col, SC)].unsqueeze(2).to_broadcast([128, SC, WIN]),
                                        ramp[:, 0:WIN].unsqueeze(1).to_broadcast([128, SC, WIN]), ALU.is_equal)
                nc.vector.tensor_tensor(onetype[:, k % 2, :, :],
                                        typ_t[:, ds(col, SC)].unsqueeze(2).to_broadcast([128, SC, R3]),
                                        ramp[:, WIN:WIN + R3].unsqueeze(1).to_broadcast([128, SC, R3]), ALU.is_equal).then_inc(onehots, 1)

            def step(a, k):
                last = isinstance(a, int) and a == STEPS - 1
                if not last:
                    if not (isinstance(a, int) and a == 0):
                        dve.wait_ge(agg_done, a * STEP_G)
                    build(a + 1, k + 1)
                if not isinstance(a, int) or a + LEAD < STEPS:
                    lay_indices(a + LEAD, (k + LEAD) % IDXR)
                g0 = (a * (-STEP_G) + (STEPS - 1) * STEP_G) if not isinstance(a, int) else (STEPS - 1 - a) * STEP_G
                starts = [dve.value_load(base_i[0:1, ds(g0 + g, 1)], min_val=0, max_val=LIVE - 1) for g in range(STEP_G)]
                for g in range(STEP_G):
                    dve.wait_ge(agg_done, a * STEP_G + (g + 1))
                    if g or not (isinstance(a, int) and a == 0):
                        dve.wait_ge(acc_added, a * STEP_G + g)
                    w = acc[:, :, ds(starts[g], WIN)]
                    got = P[g][:, 0:KT * WIN].rearrange("p (k n) -> p k n", k=KT)
                    nc.vector.tensor_tensor(w, got, w, ALU.add).then_inc(acc_added, 1)

            banded = [0]

            def take_sums(t, added):
                at_pos, at_over = [dve.value_load(where[0:1, ds(t + (banded[0] + n) * TILES, 1)], min_val=0, max_val=(LIVE - T, ZEROS)[n])
                                   for n in range(2)]
                if added is not None:
                    dve.wait_ge(acc_added, added)
                dve.nop(nofuse=True)
                first = acc[:, :, ds(at_pos, WIN)]
                link(nc.vector.tensor_tensor(first, acc[:, :, ds(at_over, WIN)], first, ALU.add), alone=True)
                sums = acc[:, :, ds(at_pos, T)]
                link(nc.vector.tensor_copy(red_h[:, :, :], sums))
                nc.vector.tensor_tensor(red_l[:, :, :], sums, red_h[:, :, :], ALU.subtract).then_inc(red_ready, 1)
                dve.wait_ge(red_ready, t + 1)
                dve.nop(nofuse=True)
                z3 = zero[:, :].unsqueeze(1)
                nc.vector.tensor_copy(acc[:, :, ds(at_pos, T)], z3.to_broadcast([128, KT, T]))
                link(nc.vector.tensor_copy(acc[:, :, ds(at_over, WIN)], z3.to_broadcast([128, KT, WIN])))

            def split_w1(c):
                dve.wait_ge(w1_high, c + 1)
                e = c * NE // W1_CUTS
                piece = slice(e, e + NE // W1_CUTS)
                nc.vector.tensor_tensor(w1l[:, piece, :, :], raw1[:, piece, :, :], w1h[:, piece, :, :], ALU.subtract).then_inc(w1_low, 1)

            def low_h(t):
                dve.wait_ge(hT_ready, t + 1)
                nc.vector.tensor_tensor(h_l[:, :, :].rearrange("p k t -> p (k t)"), P[5][:, 0:KT * T],
                                        h_h[:, :, :].rearrange("p k t -> p (k t)"), ALU.subtract).then_inc(h_l_ready, 1)

            def add_rhn(t):
                dve.wait_ge(r_ready, t + 1)
                dve.wait_ge(hn_ready, t + 1)
                nc.vector.scalar_tensor_tensor(oT[:, :, :], rT[:, :, :], 1.0, oT[:, :, :], ALU.add, ALU.mult).then_inc(rhn_ready, 1)

            def add_in(t, alone=False):
                dve.wait_ge(rhn_ready, t + 1)
                dve.wait_ge(in_done, t + 1)
                flat_o = oT[:, :, :].rearrange("p m t -> p (m t)")
                nc.vector.scalar_tensor_tensor(flat_o, flat_o, 0.5, bank("in", alone)[:, 0:KT * T], ALU.mult, ALU.add).then_inc(pre_n, 1)

            def blend_h(t):
                dve.wait_ge(n_ready, t + 1)
                link(nc.vector.tensor_tensor(oT[:, :, :], h_h[:, :, :], rT[:, :, :], ALU.subtract))
                link(nc.vector.tensor_tensor(oT[:, :, :], oT[:, :, :], h_l[:, :, :], ALU.add))

            def blend_z(t):
                dve.wait_ge(z_ready, t + 1)
                link(nc.vector.scalar_tensor_tensor(oT[:, :, :], zT[:, :, :], 1.0, oT[:, :, :], ALU.add, ALU.mult))
                nc.vector.scalar_tensor_tensor(oT[:, :, :], oT[:, :, :], 0.5, rT[:, :, :], ALU.mult, ALU.add).then_inc(gru_ready, 1)

            def residual(t):
                dve.wait_ge(gru_trans, t + 1)
                dve.wait_ge(x_loaded, t * 16 + 16)
                x1f = x1[:, :, :].rearrange("p j d -> p (j d)")
                nc.vector.tensor_tensor(x1f, P[5][0:SUB, :], x1f, ALU.add).then_inc(x1_ready, 1)
                dve.wait_ge(x1_ready, t + 1)
                for j in range(2):
                    ins = nc.vector.bn_stats(st[0:SUB, j, :], x1[:, j, :])
                link(ins, alone=True)
                for j in range(2):
                    ins = nc.vector.bn_aggr(mv[0:SUB, 0, j, :], st[0:SUB, j, :])
                link(ins)
                nc.vector.tensor_scalar_add(var[0:SUB, 0, 0:2], mv[0:SUB, 0, 0:2, 1], EPS).then_inc(var_ready, 1)

            def second_norm(t):
                dve.wait_ge(std_ready, t + 1)
                link(nc.vector.reciprocal(rstd[0:SUB, 0, 0:2], std[0:SUB, 0, 0:2]))
                for j in range(2):
                    ins = nc.vector.tensor_scalar(x2n[:, j, :], x1[:, j, :], mv[0:SUB, 0, j, 0:1], rstd[0:SUB, 0, j:j + 1],
                                                  ALU.subtract, ALU.mult)
                ins.then_inc(x2n_ready, 1)

            def low_x2(t):
                dve.wait_ge(x2h_ready, t + 1)
                nc.vector.tensor_tensor(x2l[:, :, :].rearrange("p k t -> p (k t)"), P[5][:, 0:KT * T],
                                        x2h[:, :, :].rearrange("p k t -> p (k t)"), ALU.subtract).then_inc(x2l_ready, 1)

            def gru_h(t):
                low_h(t)

            def gru(t, run):
                if banded[0]:
                    at[0], count[0] = t, links_prep[0]
                take_sums(t, FIRST_READ * STEP_G if run is not no_steps else None)
                if run is not no_steps:
                    split_w1(W1_CUTS - 1)
                add_rhn(t)
                add_in(t, True)
                blend_h(t)
                blend_z(t)
                residual(t)
                run(step, 0)
                second_norm(t)
                low_x2(t)
                links_before[0] = count[0]

            def tile(i, run, more, extra=()):
                at[0] = i
                count[0] = links_before[0]
                dve.wait_ge(scores_done, i + 1)
                halves = P[5][0:SUB, 0:4 * NE].rearrange("p (j a e) -> p j a e", j=2, a=2)
                link(nc.vector.tensor_tensor(scores[:, :, :], halves[:, :, 1, :],
                                             bgb[0:SUB, :].rearrange("p (j e) -> p j e", j=2), ALU.add))
                link(nc.vector.tensor_tensor(scores[:, :, :], halves[:, :, 0, :], scores[:, :, :], ALU.add), alone=True)
                for j in range(2):
                    ins = nc.vector.max(top[:, j, :], scores[:, j, :])
                link(ins, alone=True)
                for j in range(2):
                    ins = nc.vector.max_index(topi[:, j, :], top[:, j, :], scores[:, j, :])
                link(ins)
                link(nc.vector.tensor_copy(topf[:, :, :], topi[:, :, :]))
                for j in range(2):
                    ins = nc.vector.tensor_scalar(mask1[:, j, :], ramp[0:SUB, 0:NE], topf[:, j, 0:1], None, ALU.is_equal)
                link(ins)
                for j in range(2):
                    ins = nc.vector.scalar_tensor_tensor(mask[:, j, :, :], ramp[0:SUB, 0:NE].unsqueeze(1).to_broadcast([SUB, PARTS, NE]),
                                                         topf[:, j, 1:2], mask1[:, j, :].unsqueeze(1).to_broadcast([SUB, PARTS, NE]),
                                                         ALU.is_equal, ALU.add)
                ins.then_inc(mask_ready, 1)
                dve.wait_ge(mask_ready, i + 1)

                def add_expert(e):
                    dve.wait_ge(l2_done, i * NE + (e + 1))
                    if e:
                        dve.wait_ge(moe_added, i * NE + e)
                    for j in range(2):
                        ins = nc.vector.scalar_tensor_tensor(y[:, j, :], P[7 - e % 2][0:SUB, j * D:(j + 1) * D],
                                                             mask[:, j, 0, e:e + 1], y[:, j, :], ALU.mult, ALU.add)
                    ins.then_inc(moe_added, 1)

                run(step, 0)
                dve.wait_ge(b2_done, i + 1)
                dve.wait_ge(y_moved, i * 16 + 16 * 3)
                nc.vector.tensor_tensor(y[:, :, :].rearrange("p j d -> p (j d)"), P[5][0:SUB, :],
                                        x1[:, :, :].rearrange("p j d -> p (j d)"), ALU.add).then_inc(y_ready, 1)
                dve.wait_ge(y_ready, i + 1)
                add_expert(0)
                for e in range(1, NE):
                    if more and e == 5:
                        add_in(i + 1)
                        blend_h(i + 1)
                    run(step, e)
                    if more and e == 1:
                        low_h(i + 1)
                    if more and e == READ_AT - 1:
                        for k in extra:
                            step(i * SLOTS + FIRST + k, FIRST + k)
                        take_sums(i + 1, i * (SLOTS * STEP_G) + (FIRST + READ_AT + len(extra)) * STEP_G)
                    if more and e == 4:
                        add_rhn(i + 1)
                    if more and e == 5:
                        blend_z(i + 1)
                    if more and e == 6:
                        second_norm(i + 1)
                    if more and e == 7:
                        low_x2(i + 1)
                    add_expert(e)
                    if more and e == 5:
                        residual(i + 1)
                dve.wait_ge(moe_added, i * NE + NE)
                assert not more or count[0] == links_before[0] + LINKS, count[0] - links_before[0]

            links_before = [0]

            def fast():
                for a in range(LEAD):
                    lay_indices(a, a)
                build(0, 0)
                small_weights()
                links_prep[0] = count[0]
                tile_loop(dve, step, gru_h, gru, tile, split_w1)

            def general():
                at[0], banded[0] = 0, 2
                count[0] = links_before_paths
                small_weights()
                assert count[0] == links_prep[0]
                for c in range(W1_CUTS):
                    split_w1(c)
                nc.vector.tensor_scalar_add(ramp_w[:, :], ramp[:, 0:WIN], float(N - BT * T)).then_inc(g_ramp, 1)

                def sum_band(b):
                    first_s = b * STEPS
                    with dve.Fori(0, STEPS // RING_S) as q:
                        dve.nop(nofuse=True)
                        nc.vector.tensor_copy(idx[:, 0:RING_S, :].rearrange("p r c -> p (r c)"),
                                              src_t[:, ds(q * (RING_S * SC), RING_S * SC)]).then_inc(g_idx, 1)
                        with dve.Fori(0, RING_S) as r:
                            s = q * RING_S + r
                            nc.vector.tensor_tensor(onetype[:, 0, :, :],
                                                    typ_t[:, ds(s * SC, SC)].unsqueeze(2).to_broadcast([128, SC, R3]),
                                                    ramp[:, WIN:WIN + R3].unsqueeze(1).to_broadcast([128, SC, R3]), ALU.is_equal).then_inc(g_type, 1)
                            with dve.Fori(0, BW) as w:
                                v = (first_s + s) * BW + w
                                moved = (first_s + s) * (BW + 1) + w + b + 1
                                dve.wait_ge(g_ramp, moved)
                                nc.vector.tensor_tensor(onehot[:, 0, :, :],
                                                        dst_t[:, ds(s * SC, SC)].unsqueeze(2).to_broadcast([128, SC, WIN]),
                                                        ramp_w[:, :].unsqueeze(1).to_broadcast([128, SC, WIN]), ALU.is_equal).then_inc(g_onehot, 1)
                                dve.wait_ge(g_onehot, v + 1)
                                nc.vector.tensor_scalar_add(ramp_w[:, :], ramp_w[:, :], float(WIN)).then_inc(g_ramp, 1)
                                dve.wait_ge(g_agg, v + 1)
                                win = acc[:, :, ds(w * WIN, WIN)]
                                for g in range(STEP_G):
                                    if g:
                                        dve.wait_ge(g_half, v + 1)
                                    got = P[g][:, 0:KT * WIN].rearrange("p (k n) -> p k n", k=KT)
                                    nc.vector.tensor_tensor(win, got, win, ALU.add).then_inc((g_half, g_added)[g], 1)
                                dve.wait_ge(g_added, v + 1)
                            dve.wait_ge(g_ramp, (first_s + s) * (BW + 1) + b + (BW + 1))
                            nc.vector.tensor_scalar_add(ramp_w[:, :], ramp_w[:, :], -float(BW * WIN)).then_inc(g_ramp, 1)
                    dve.wait_ge(g_ramp, (first_s + STEPS) * (BW + 1) + b + 1)
                    nc.vector.tensor_scalar_add(ramp_w[:, :], ramp_w[:, :], -float(BT * T)).then_inc(g_ramp, 1)

                by_bands(dve, sum_band, gru_h, gru, tile)

            links_prep = [0]
            links_before_paths = count[0]
            paths(dve, fast, general)

        @block.tensor
        def _(pe):
            pe.wait_ge(s_ones, 1)
            pe.wait_ge(s_viol, 1)
            nc.tensor.matmul(P[0][:, 0:1], ones[:, :], vsum[:, :], start=True, stop=True).then_inc(s_violb, 1)
            pe.wait_ge(s_diag, 1)
            nc.tensor.matmul(P[1][:, :], ones[:, :], diag, start=True, stop=True).then_inc(s_baseb, 1)
            q = 0

            def bank_free(q):
                if q >= 4:
                    pe.wait_ge(s_dst_out if q < 4 + RT else s_tr_out, q - 3 if q < 4 + RT else q - 3 - RT)

            for n in range(3):
                if n:
                    pe.wait_ge(s_natf, n)
                for r in range(RT):
                    bank_free(q)
                    for j in range(GC):
                        ins = nc.tensor.transpose(P[2 + q % 4][:, j * 128:(j + 1) * 128], nat[:, n, r, j * 128:(j + 1) * 128], ident[:, :])
                    ins.then_inc(s_tr, 1)
                    q += 1
            pe.wait_ge(s_wnat, 16 * 5)
            for n in range(2):
                for m in range(3):
                    wq = q - 3 * RT
                    if wq >= 2:
                        bank_free(q + 2)
                    for k in range(KT):
                        for b in range(2):
                            at = k * 256 + b * 128
                            ins = nc.tensor.transpose(P[(6, 7, 2, 3, 4, 5)[wq]][:, at:at + 128], wnat[:, n, 2 * m + b, k * 128:(k + 1) * 128], ident[:, :])
                    ins.then_inc(s_tr, 1)
                    q += 1
            nc.tensor.transpose(P[1][:, 0:44], bias_rows[:, :], ident[0:44, 0:44]).then_inc(s_bias, 1)
            pe.wait_ge(s_tr_out, q - RT)
            pe.wait_ge(s_weights, 16 * 6)

            def products(r, k, g):
                for f in range(KT):
                    to = P[g][:, f * WIN:(f + 1) * WIN]
                    for part in range(PARTS):
                        at = part * D + f * 128
                        for j in range(GC):
                            nc.tensor.matmul(to, ring[:, r * STEP_G + g, j, at:at + 128], onehot[:, k, g * GC + j, :],
                                             start=(part == 0 and j == 0), stop=False)
                    ins = nc.tensor.matmul(to, rels[:, f * 128:(f + 1) * 128], cts[:, g * WIN:(g + 1) * WIN],
                                           start=False, stop=True)
                return ins

            def relation_counts(k):
                for g in range(STEP_G):
                    to = P[0][0:R3, 256 + g * WIN:256 + (g + 1) * WIN]
                    for j in range(GC):
                        ins = nc.tensor.matmul(to, onetype[:, k, g * GC + j, :], onehot[:, k, g * GC + j, :],
                                               start=(j == 0), stop=(j == GC - 1))
                return ins

            def sums(a, k):
                pe.wait_ge(cts_ready, a + 1)
                for g in range(STEP_G):
                    r = k % RING_S
                    fills = (a // RING_S + 1) if isinstance(a, int) else None
                    if fills is None:
                        pe.wait_ge(gathered[r * STEP_G + g], (a - k) * (16 * GC // RING_S) + 16 * GC * (k // RING_S + 1))
                    else:
                        pe.wait_ge(gathered[r * STEP_G + g], 16 * GC * fills)
                    if g == 0 and not (isinstance(a, int) and a == 0):
                        pe.wait_ge(acc_added, a * STEP_G)
                    products(r, k % 2, g).then_inc(agg_done, 1)

            def next_counts(a, k):
                if not (isinstance(a, int) and a == STEPS - 1):
                    pe.wait_ge(onehots, a + 2)
                    pe.wait_ge(acc_added, a * STEP_G + 1)
                    relation_counts((k + 1) % 2).then_inc(counts_done, 1)

            def step(a, k):
                sums(a, k)
                next_counts(a, k)

            def transpose_h(t, before=None):
                pe.wait_ge(h_loaded, t * 16 + 16)
                if before:
                    before()
                for k in range(KT):
                    for j in range(2):
                        at = k * T + j * SUB
                        for part in range(PARTS):
                            ins = nc.tensor.matmul(P[5][:, at:at + SUB], h_in[:, j, part * D + k * 128:part * D + (k + 1) * 128],
                                                   ident16[0:SUB, 0:SUB], start=(part == 0), stop=(part == PARTS - 1))
                ins.then_inc(h_trans, 1)

            def gate(to_bank, row, which):
                halves = {"h": ((whh_h, h_h), (whh_h, h_l), (whh_l, h_h)),
                          "x": ((wih_h, red_h), (wih_h, red_l), (wih_l, red_h))}
                for m in range(KT):
                    to = to_bank[:, m * T:(m + 1) * T]
                    ops = [(a, b, k) for w in which for k in range(KT) for a, b in halves[w]]
                    for n, (a, b, k) in enumerate(ops):
                        ins = nc.tensor.matmul(to, a[:, k, row + m * 128:row + (m + 1) * 128], b[:, k, :],
                                               start=(n == 0), stop=(n == len(ops) - 1))
                return ins

            def gate_hn(t, alone=False):
                pe.wait_ge(h_l_ready, t + 1)
                gate(bank("hn", alone), 2 * D, "h").then_inc(hn_done, 1)

            def gate_r(t, alone=False):
                pe.wait_ge(red_ready, t + 1)
                if not alone:
                    pe.wait_ge(hn_ready, t + 1)
                gate(bank("r", alone), 0, "hx").then_inc(r_done, 1)

            def gate_z(t, alone=False):
                if not alone:
                    pe.wait_ge(pre_n, t + 1)
                gate(bank("z", alone), D, "hx").then_inc(z_done, 1)

            def gate_in(t, alone=False):
                if not alone:
                    pe.wait_ge(r_ready, t + 1)
                gate(bank("in", alone), 2 * D, "x").then_inc(in_done, 1)

            def transpose_gru(t):
                pe.wait_ge(gru_ready, t + 1)
                for j in range(2):
                    for k in range(KT):
                        at = j * D + k * 128
                        ins = nc.tensor.transpose(P[5][0:SUB, at:at + 128], oT[:, k, j * SUB:(j + 1) * SUB], ident[:, :])
                ins.then_inc(gru_trans, 1)

            def transpose_x2(t):
                pe.wait_ge(x2n_ready, t + 1)
                for k in range(KT):
                    for j in range(2):
                        at = k * T + j * SUB
                        ins = nc.tensor.transpose(P[5][:, at:at + SUB], x2n[:, j, k * 128:(k + 1) * 128], ident[0:SUB, 0:SUB])
                ins.then_inc(x2_trans, 1)

            def gru_h(t):
                transpose_h(t)
                gate_hn(t, True)

            def gru(t, run):
                gate_r(t, True)
                gate_in(t, True)
                gate_z(t, True)
                run(sums, 0)
                transpose_gru(t)
                run(next_counts, 0)
                transpose_x2(t)
                pe.wait_ge(w1_low, W1_CUTS)

            def tile(i, run, more, extra=()):
                pe.wait_ge(x2l_ready, i + 1)
                for j in range(2):
                    ops = [(a, k) for k in range(KT) for a in (x2h, x2l)]
                    for n, (a, k) in enumerate(ops):
                        ins = nc.tensor.matmul(P[5][0:SUB, j * 2 * NE:(j + 1) * 2 * NE], a[:, k, j * SUB:(j + 1) * SUB],
                                               wghl[:, k, :, :].rearrange("p a e -> p (a e)"), start=(n == 0), stop=(n == len(ops) - 1))
                ins.then_inc(scores_done, 1)

                def layer1(e):
                    for s in range(HS):
                        p = e * (HS // 2) + s // 2
                        if s % 2 == 0:
                            if p >= 3:
                                pe.wait_ge(gelu_done, i * PAIRS + (p - 2))
                        to = P[2 + p % 3][:, (s % 2) * T:(s % 2 + 1) * T]
                        ops = [(a, b, k) for k in range(KT) for a, b in ((w1h, x2h), (w1h, x2l), (w1l, x2h))]
                        for n, (a, b, k) in enumerate(ops):
                            ins = nc.tensor.matmul(to, a[:, e, k, s * 128:(s + 1) * 128], b[:, k, :],
                                                   start=(n == 0), stop=(n == len(ops) - 1))
                        if s % 2:
                            ins.then_inc(l1_done, 1)

                def layer2(e):
                    if e >= 2:
                        pe.wait_ge(moe_added, i * NE + (e - 1))
                    pe.wait_ge(gelu_done, i * PAIRS + (e + 1) * (HS // 2))
                    for j in range(2):
                        to = P[7 - e % 2][0:SUB, j * D:(j + 1) * D]
                        for s in range(HS):
                            ins = nc.tensor.matmul(to, gT[:, e % 2, s, j * SUB:(j + 1) * SUB], w2[:, e, s, :],
                                                   start=(s == 0), stop=(s == HS - 1))
                    ins.then_inc(l2_done, 1)

                layer1(0)
                pe.wait_ge(mask_ready, i + 1)
                for j in range(2):
                    ins = nc.tensor.transpose(P[5][0:NE3, 64 + j * SUB:64 + (j + 1) * SUB], mask[:, j, :, :].rearrange("p a e -> p (a e)"), ident[0:SUB, 0:SUB])
                ins.then_inc(mask_trans, 1)
                layer1(1)
                run(sums, 0)
                pe.wait_ge(s_experts, 16 * W1_CUTS)
                layer2(0)
                pe.wait_ge(maskT_ready, i + 1)
                for j in range(2):
                    ins = nc.tensor.matmul(P[5][0:SUB, j * D:(j + 1) * D], maskT[:, j * SUB:(j + 1) * SUB], b2s[:, :],
                                           start=True, stop=True)
                ins.then_inc(b2_done, 1)
                run(next_counts, 0)
                for e in range(1, NE):
                    if e + 1 < NE:
                        layer1(e + 1)
                    if more and e == 4:
                        gate_r(i + 1)
                    if more and e == 5:
                        gate_z(i + 1)
                    if more and e == 7:
                        transpose_x2(i + 1)
                    run(sums, e)
                    if more and e == 1:
                        transpose_h(i + 1, lambda: pe.wait_ge(y_ready, i + 1))
                    if more and e == 2:
                        gate_hn(i + 1)
                    layer2(e)
                    run(next_counts, e)
                    if e == READ_AT - 1:
                        for k in extra:
                            step(i * SLOTS + FIRST + k, FIRST + k)
                    if more and e == 4:
                        gate_in(i + 1)
                    if more and e == 5:
                        transpose_gru(i + 1)

            def fast():
                pe.wait_ge(s_small, 1)
                pe.wait_ge(onehots, 1)
                relation_counts(0).then_inc(counts_done, 1)
                tile_loop(pe, step, gru_h, gru, tile)

            def general():
                pe.wait_ge(s_small, 1)

                def sum_band(b):
                    with pe.Fori(0, STEPS // RING_S) as q:
                        n = b * (STEPS // RING_S) + q
                        for r in range(RING_S):
                            for g in range(STEP_G):
                                pe.wait_ge(gathered[r * STEP_G + g], n * (16 * GC) + 16 * GC)
                            s = n * RING_S + r
                            pe.wait_ge(g_type, s + 1)
                            pe.nop(nofuse=True)
                            with pe.Fori(0, BW) as w:
                                v = s * BW + w
                                pe.wait_ge(g_onehot, v + 1)
                                relation_counts(0).then_inc(g_counts, 1)
                                pe.wait_ge(g_cts, v + 1)
                                products(r, 0, 0)
                                products(r, 0, 1).then_inc(g_agg, 1)

                by_bands(pe, sum_band, gru_h, gru, tile)

            paths(pe, fast, general)


_INS = ["x", "src", "dst", "edge_type_16", "L0_gnn_relvectors", "L0_gnn_w_ih", "L0_gnn_w_hh", "L0_gnn_b_ih",
        "L0_gnn_b_hh", "L0_ffn_Wg", "L0_ffn_bg", "L0_ffn_W1", "L0_ffn_b1", "L0_ffn_W2", "L0_ffn_b2"]


def kernel(**inputs):
    import numpy as _np
    import concourse.bacc as _bacc
    from concourse import mybir as _mybir
    from concourse.bass_utils import run_bass_kernel_spmd as _run

    nc = _bacc.Bacc("TRN2", target_bir_lowering=False, num_devices=1)
    arrays, args = {}, []
    named = [(n, _np.ascontiguousarray(inputs[n])) for n in _INS]
    named += list(zip(("c_ident", "c_ramp", "c_cols", "c_where"), shape_constants()))
    for name, a in named:
        arrays[f"in_{name}_dram"] = a
        args.append(nc.dram_tensor(f"in_{name}_dram", a.shape, _mybir.dt.from_np(a.dtype), kind="ExternalInput").ap())
    out = nc.dram_tensor("out_0_dram", (N, D), _mybir.dt.float32, kind="ExternalOutput").ap()
    gnn_ffn_kernel(nc, *args, out)
    r = _run(nc, [arrays], core_ids=[0])
    return r.results[0]["out_0_dram"]
```
